# Optimizing a Trainium2 kernel written in Bass

```python
import numpy as np
import jax
import jax.numpy as jnp

def _softmax(x, axis=-1):
    return jax.nn.softmax(x, axis=axis)

def _gelu(x):
    return jax.nn.gelu(x, approximate=True)

def _silu(x):
    return jax.nn.silu(x)

def _sigmoid(x):
    return jax.nn.sigmoid(x)

def _layernorm(x, axis=-1, eps=1e-05):
    m = jnp.mean(x, axis=axis, keepdims=True)
    v = jnp.var(x, axis=axis, keepdims=True)
    return (x - m) / jnp.sqrt(v + eps)

def _scatter_add(tgt, idx, src, axis=0):
    return tgt.at[idx].add(src)

def _segment_sum(src, seg, n):
    return jax.ops.segment_sum(src, seg, n)
kernel_name = 'mk_cond_seq_d1_seqx_r4_32abf0'

def setup_inputs(seed: int=0):
    np.random.seed(seed)
    _w = jnp.asarray

    def _rec_inputs():
        import jax
        import jax.numpy as jnp
        _rk = jax.random.key(seed)
        x = -0.0002928 + 1 * jax.random.normal(jax.random.fold_in(_rk, 1), (4, 512, 256), jnp.float32)
        _lenS = 512 - jax.random.randint(jax.random.fold_in(_rk, 7), (4,), 0, max(1, 512 // 4) + 1, jnp.int32)
        _lenS2 = 512 - jax.random.randint(jax.random.fold_in(_rk, 8), (4,), 0, max(1, 512 // 4) + 1, jnp.int32)
        cond_1024 = 0.0061147 + 1.02565 * jax.random.normal(jax.random.fold_in(_rk, 11), (4, 256), jnp.float32)
        return (x, cond_1024)
    x, cond_1024 = _rec_inputs()

    def _L0_cond_setup():
        import jax, jax.numpy as jnp
        import numpy as np
        B, T, DIM = (4, 256, 256)
        COND = 256
        HEADS, DH = (16, 64)
        INNER = HEADS * DH
        MLP = 1024
        EPS = 1e-05

        def _layernorm(x):
            mu = jnp.mean(x, axis=-1, keepdims=True)
            var = jnp.mean(jnp.square(x - mu), axis=-1, keepdims=True)
            return (x - mu) * jax.lax.rsqrt(var + EPS)

        def _modulate(x, shift, scale):
            return x * (1.0 + scale) + shift

        def _attention(x, W_qkv, W_out, b_out):
            Bq, Tq, _ = x.shape
            qkv = x @ W_qkv
            q, k, v = jnp.split(qkv, 3, axis=-1)
            q = q.reshape(Bq, Tq, HEADS, DH)
            k = k.reshape(Bq, Tq, HEADS, DH)
            v = v.reshape(Bq, Tq, HEADS, DH)
            scale = DH ** (-0.5)
            attn = jnp.einsum('bqhd,bkhd->bhqk', q, k) * scale
            attn = jax.nn.softmax(attn, axis=-1)
            out = jnp.einsum('bhqk,bkhd->bqhd', attn, v).reshape(Bq, Tq, INNER)
            return out @ W_out + b_out

        def _ff(x, W1, b1, W2, b2):
            return jax.nn.gelu(x @ W1 + b1, approximate=False) @ W2 + b2
        key = jax.random.key(seed)
        ks = jax.random.split(key, 12)
        s = 0.02
        return {'x': jax.random.normal(ks[0], (B, T, DIM), jnp.float32), 'c': jax.random.normal(ks[1], (B, 1, COND), jnp.float32), 'W_mod': jax.random.normal(ks[2], (COND, 6 * DIM), jnp.float32) * s, 'b_mod': jax.random.normal(ks[3], (6 * DIM,), jnp.float32) * s, 'W_qkv': jax.random.normal(ks[4], (DIM, 3 * INNER), jnp.float32) * s, 'W_out': jax.random.normal(ks[5], (INNER, DIM), jnp.float32) * s, 'b_out': jax.random.normal(ks[6], (DIM,), jnp.float32) * s, 'W1': jax.random.normal(ks[7], (DIM, MLP), jnp.float32) * s, 'b1': jax.random.normal(ks[8], (MLP,), jnp.float32) * s, 'W2': jax.random.normal(ks[9], (MLP, DIM), jnp.float32) * s, 'b2': jax.random.normal(ks[10], (DIM,), jnp.float32) * s}
    _L0_cond_all = _L0_cond_setup()
    _L0_cond_in = {k: v for k, v in _L0_cond_all.items() if k in ('W_mod', 'b_mod', 'W_qkv', 'W_out', 'b_out', 'W1', 'b1', 'W2', 'b2')}
    del _L0_cond_all
    return {'x': x, 'cond_1024': cond_1024, 'L0_cond_W_mod': _L0_cond_in['W_mod'], 'L0_cond_b_mod': _L0_cond_in['b_mod'], 'L0_cond_W_qkv': _L0_cond_in['W_qkv'], 'L0_cond_W_out': _L0_cond_in['W_out'], 'L0_cond_b_out': _L0_cond_in['b_out'], 'L0_cond_W1': _L0_cond_in['W1'], 'L0_cond_b1': _L0_cond_in['b1'], 'L0_cond_W2': _L0_cond_in['W2'], 'L0_cond_b2': _L0_cond_in['b2']}

def reference(x, cond_1024, L0_cond_W_mod, L0_cond_b_mod, L0_cond_W_qkv, L0_cond_W_out, L0_cond_b_out, L0_cond_W1, L0_cond_b1, L0_cond_W2, L0_cond_b2):
    import jax
    import jax.numpy as jnp

    def _L0_cond_ref(x, c, W_mod, b_mod, W_qkv, W_out, b_out, W1, b1, W2, b2):
        import jax, jax.numpy as jnp
        import numpy as np
        B, T, DIM = (4, 256, 256)
        COND = 256
        HEADS, DH = (16, 64)
        INNER = HEADS * DH
        MLP = 1024
        EPS = 1e-05

        def _layernorm(x):
            mu = jnp.mean(x, axis=-1, keepdims=True)
            var = jnp.mean(jnp.square(x - mu), axis=-1, keepdims=True)
            return (x - mu) * jax.lax.rsqrt(var + EPS)

        def _modulate(x, shift, scale):
            return x * (1.0 + scale) + shift

        def _attention(x, W_qkv, W_out, b_out):
            Bq, Tq, _ = x.shape
            qkv = x @ W_qkv
            q, k, v = jnp.split(qkv, 3, axis=-1)
            q = q.reshape(Bq, Tq, HEADS, DH)
            k = k.reshape(Bq, Tq, HEADS, DH)
            v = v.reshape(Bq, Tq, HEADS, DH)
            scale = DH ** (-0.5)
            attn = jnp.einsum('bqhd,bkhd->bhqk', q, k) * scale
            attn = jax.nn.softmax(attn, axis=-1)
            out = jnp.einsum('bhqk,bkhd->bqhd', attn, v).reshape(Bq, Tq, INNER)
            return out @ W_out + b_out

        def _ff(x, W1, b1, W2, b2):
            return jax.nn.gelu(x @ W1 + b1, approximate=False) @ W2 + b2
        mod = jax.nn.silu(c) @ W_mod + b_mod
        sh_msa, sc_msa, g_msa, sh_mlp, sc_mlp, g_mlp = jnp.split(mod, 6, axis=-1)
        x = x + g_msa * _attention(_modulate(_layernorm(x), sh_msa, sc_msa), W_qkv, W_out, b_out)
        x = x + g_mlp * _ff(_modulate(_layernorm(x), sh_mlp, sc_mlp), W1, b1, W2, b2)
        return x
    x = _L0_cond_ref(x, cond_1024[:, None, :], L0_cond_W_mod, L0_cond_b_mod, L0_cond_W_qkv, L0_cond_W_out, L0_cond_b_out, L0_cond_W1, L0_cond_b1, L0_cond_W2, L0_cond_b2)
    return x

_drawn_inputs = setup_inputs


def setup_inputs(seed=0):
    import zlib

    import numpy as np

    out = dict(_drawn_inputs(seed))
    spreads = {}
    factors = {'L0_cond_b_mod': 8.0,
     'L0_cond_W_qkv': 6.884,
     'L0_cond_W_out': 6.574,
     'L0_cond_b_out': 22.037,
     'L0_cond_b1': 64.0,
     'L0_cond_b2': 21.922,
     'L0_cond_W1': 4.042,
     'L0_cond_W2': 3.632}
    for name, (base, spread) in spreads.items():
        noise = np.random.default_rng([zlib.crc32(name.encode()), seed]).standard_normal(out[name].shape)
        drawn = base * np.exp(spread * noise) if base else spread * noise
        out[name] = jnp.asarray(drawn.astype(out[name].dtype))
    for name, factor in factors.items():
        out[name] = (out[name] * factor).astype(out[name].dtype)
    return out
```

```python
from contextlib import ExitStack

import concourse.bass as bass
from concourse import mybir

F32 = mybir.dt.float32
F16 = mybir.dt.float16
I32 = mybir.dt.int32
ACT = mybir.ActivationFunctionType
ALU = mybir.AluOpType
AX = mybir.AxisListType

P = 128
EPS = 1e-5
WS = 64.0
RSQRT_MAGIC = 1597463007.0


def dit_block_kernel(nc, x, cond, W_mod, b_mod, W_qkv, W_out, b_out, W1, b1, W2, b2, out):
    B, T, D = x.shape
    COND = cond.shape[1]
    INNER = W_out.shape[0]
    MLP = W1.shape[1]
    DH = 64
    PAIRS = INNER // (2 * DH)
    NP = B * PAIRS
    QT = T // P
    KC = T // P
    DC = D // P
    CC = COND // P
    FC = MLP // P
    NT = B * QT
    assert T == 512 and D == 256 and COND == 256 and 2 * DH == P and QT == 4

    x_tiles = x.rearrange("b (t p) d -> p b t d", p=P)
    out_tiles = out.rearrange("b (t p) d -> p b t d", p=P)

    with ExitStack() as ctx:
        def sb(name, shape, dt):
            return ctx.enter_context(nc.sbuf_tensor(name, shape, dt))

        def sem(name):
            return ctx.enter_context(nc.semaphore(name))

        wqkv_hi = sb("wqkv_hi", [P, DC, 3, PAIRS, P], F16)
        wqkv_lo = sb("wqkv_lo", [P, DC, 3, PAIRS, P], F16)
        wout_hi = sb("wout_hi", [P, PAIRS, D], F16)
        wout_lo = sb("wout_lo", [P, PAIRS, D], F16)
        w1_hi = sb("w1_hi", [P, DC, MLP], F16)
        w1_lo = sb("w1_lo", [P, DC, MLP], F16)
        w2_hi = sb("w2_hi", [P, FC, D], F16)
        w2_lo = sb("w2_lo", [P, FC, D], F16)
        bias_rows = sb("bias_rows", [P, 2, D], F16)
        ones = sb("ones", [P, P], F16)
        ident = sb("ident", [P, P], F32)
        gates = sb("gates", [P, B, 2, D], F32)
        modT = sb("modT", [P, 8, B], F32)
        b1_col = sb("b1_col", [P, FC], F32)
        bmod_col = sb("bmod_col", [P, 6 * DC], F32)
        xnT_hi = sb("xnT_hi", [P, DC, B, T], F16)
        xnT_lo = sb("xnT_lo", [P, DC, B, T], F16)
        stats = sb("stats", [P, NT, 6], F32)
        mv = sb("mv", [P, NT, 2], F32)
        var = sb("var", [P, NT], F32)
        rstd = sb("rstd", [P, NT], F32)
        newton = sb("newton", [P, NT], F32)
        cond_sb = sb("cond_sb", [B, COND], F32)
        exp_c = sb("exp_c", [P, CC, B], F32)
        silu_c = sb("silu_c", [P, CC, B], F32)
        wait_bearer = sb("wait_bearer", [P, 1], F32)
        recip = sb("recip", [P, QT, 2], F32)
        one = sb("one", [P, 1], F32)
        neg_max = sb("neg_max", [P, 2, 2], F32)
        sums = sb("sums", [P, 2, QT, 2], F32)

        r1 = sb("r1", [P, 2 * NP * T], F16)
        o_hi = r1[:, 0:NP * T].rearrange("p (b h t) -> p b h t", b=B, h=PAIRS)
        o_lo = r1[:, NP * T:2 * NP * T].rearrange("p (b h t) -> p b h t", b=B, h=PAIRS)
        r1f = r1[:, :].bitcast(F32)
        at = [0]

        def stage(n):
            at[0] += n
            return r1f[:, at[0] - n:at[0]]

        wqkv_raw = stage(DC * 3 * INNER)
        wmod_raw = stage(CC * 6 * D).rearrange("p (c n) -> p c n", c=CC)
        wout_raw = stage(PAIRS * D)
        w1_raw = stage(DC * MLP)
        w2_raw = stage(FC * D)

        r2 = sb("r2", [P, 2 * 2 * 2 * KC * T], F16)
        probsT_hi = r2[:, 0:16 * T].rearrange("p (u h k q) -> p u h k q", u=2, h=2, k=KC)
        probsT_lo = r2[:, 16 * T:32 * T].rearrange("p (u h k q) -> p u h k q", u=2, h=2, k=KC)
        r2f = r2[:, :].bitcast(F32)
        x_all = r2f[:, 0:NT * D].rearrange("p (b t d) -> p b t d", b=B, t=QT)
        mod1 = r2f[:, NT * D:NT * D + 2 * T].rearrange("p (u t) -> p u t", u=2)
        silu_rep = r2f[:, NT * D + 2 * T:NT * D + 2 * T + CC * B * P].rearrange("p (c b m) -> p c b m", c=CC, b=B)
        bmod_rep = r2f[:, NT * D + 4 * T:NT * D + 5 * T].rearrange("p (g d) -> p g d", g=2)
        bias_raw = r2f[:, NT * D + 5 * T:NT * D + 6 * T].rearrange("p (g d) -> p g d", g=2)
        bias_hi = r2[:, 2 * (NT * D + 6 * T):2 * (NT * D + 6 * T) + 2 * D].rearrange("p (g d) -> p g d", g=2)
        h_hi = r2[:, 2 * NT * D:2 * NT * D + FC * T].rearrange("p (f t) -> p f t", f=FC)
        h_lo = r2[:, 2 * NT * D + FC * T:2 * NT * D + 2 * FC * T].rearrange("p (f t) -> p f t", f=FC)

        r3 = sb("r3", [P, 2, 2, T], F32)
        probs = r3
        mod2 = r3[:, 0, :, :]
        gelu_out = r3[:, 1, :, :]

        r4 = sb("r4", [P, 16 * T], F16)
        q2 = r4[:, 0:4 * T].rearrange("p (u h t) -> p u h t", u=2, h=2)
        k2_hi = r4[:, 4 * T:8 * T].rearrange("p (u h t) -> p u h t", u=2, h=2)
        k2_lo = r4[:, 8 * T:12 * T].rearrange("p (u h t) -> p u h t", u=2, h=2)
        q_hi, q_lo, k_hi, k_lo = (r4[:, (12 + i) * T:(13 + i) * T] for i in range(4))
        r4f = r4[:, :].bitcast(F32)
        xn2 = r4f[:, 0:2 * T].rearrange("p (t d) -> p t d", t=QT)
        scaled = r4f[:, 2 * T:4 * T].rearrange("p (h t d) -> p h t d", h=2, t=2)
        xn2T_hi = r4[:, 8 * T:10 * T].rearrange("p (c t) -> p c t", c=DC)
        xn2T_lo = r4[:, 10 * T:12 * T].rearrange("p (c t) -> p c t", c=DC)

        v_hi = sb("v_hi", [P, 2, KC, P], F16)
        v_lo = sb("v_lo", [P, 2, KC, P], F16)
        recip_rep = sb("recip_rep", [P, QT, 2, DH], F32)
        o_norm = sb("o_norm", [P, 2, T], F32)

        ps_scores = [ctx.enter_context(nc.psum_tensor(f"ps_scores{i}", [P, 2, T], F32)) for i in range(2)]
        ps_turn = ctx.enter_context(nc.psum_tensor("ps_turn", [P, 2, T], F32))
        ps_proj = ctx.enter_context(nc.psum_tensor("ps_proj", [P, T], F32))
        ps_vals = ctx.enter_context(nc.psum_tensor("ps_vals", [P, T], F32))
        ps_attn = ps_scores[0][:, :, :].rearrange("p k (t d) -> p k t d", t=2)
        ps_mlp = ps_scores[1][:, :, :].rearrange("p k (t d) -> p k t d", t=2)
        ps_hid = [ps_proj, ps_vals]

        cond_loaded = sem("cond_loaded")
        wmod_loaded = sem("wmod_loaded")
        x_loaded = [sem(f"x_loaded{b}") for b in range(B)]
        wqkv_loaded = sem("wqkv_loaded")
        wrest_loaded = sem("wrest_loaded")
        small_loaded = sem("small_loaded")
        consts_ready = sem("consts_ready")
        cond_turned = sem("cond_turned")
        exp_c_ready = sem("exp_c_ready")
        silu_ready = sem("silu_ready")
        mod_made = sem("mod_made")
        modT_ready = sem("modT_ready")
        gates_made = sem("gates_made")
        gates_read = sem("gates_read")
        xn_ready = sem("xn_ready")
        xn_turned = sem("xn_turned")
        mod1_ready = sem("mod1_ready")
        xnT_hi_ready = sem("xnT_hi_ready")
        xnT_lo_ready = sem("xnT_lo_ready")
        wqkv_hi_ready = sem("wqkv_hi_ready")
        wqkv_lo_ready = sem("wqkv_lo_ready")
        wrest_step = sem("wrest_step")
        wrest_ready = sem("wrest_ready")
        bias_hi_ready = sem("bias_hi_ready")
        bias_ready = sem("bias_ready")
        dve_chain = sem("dve_chain")
        k_made, k_hi_ready, k_lo_ready, k_spread = (sem(n) for n in ("k_made", "k_hi_ready", "k_lo_ready", "k_spread"))
        q_made, q_hi_ready, q_lo_ready, q_spread = (sem(n) for n in ("q_made", "q_hi_ready", "q_lo_ready", "q_spread"))
        v_made, v_hi_ready, v_lo_ready = (sem(n) for n in ("v_made", "v_hi_ready", "v_lo_ready"))
        scores_made = sem("scores_made")
        max_ready = sem("max_ready")
        probs_ready = sem("probs_ready")
        turned = sem("turned")
        turn_hi_ready = sem("turn_hi_ready")
        turn_lo_ready = sem("turn_lo_ready")
        vals_made = sem("vals_made")
        recip_ready = sem("recip_ready")
        recip_rep_ready = sem("recip_rep_ready")
        recip_turned = sem("recip_turned")
        recip_T_ready = sem("recip_T_ready")
        o_norm_ready = sem("o_norm_ready")
        o_hi_ready = sem("o_hi_ready")
        o_lo_ready = sem("o_lo_ready")
        xr_loaded = sem("xr_loaded")
        attn_made = sem("attn_made")
        attn_read = sem("attn_read")
        xn2_ready = sem("xn2_ready")
        xn2_turned = sem("xn2_turned")
        mod2_ready = sem("mod2_ready")
        xn2T_hi_ready = sem("xn2T_hi_ready")
        xn2T_lo_ready = sem("xn2T_lo_ready")
        hid_made = sem("hid_made")
        gelu_ready = sem("gelu_ready")
        h_hi_ready = sem("h_hi_ready")
        h_lo_ready = sem("h_lo_ready")
        mlp_made = sem("mlp_made")
        mlp_read = sem("mlp_read")
        y_ready = sem("y_ready")
        stored = sem("stored")

        def over_pairs(eng, pair):
            pair(0, 0)
            pair(1, 1)
            with eng.Fori(1, NP // 2 - 1) as i:
                pair(2 * i, 0)
                pair(2 * i + 1, 1)
            for j in (NP - 2, NP - 1, NP, NP + 1):
                pair(j, j % 2)

        def exists(j, back=0, ahead=0):
            return not isinstance(j, int) or 0 <= j - back + ahead < NP

        def over_batches(eng, body):
            body(0, False, False)
            with eng.Fori(1, B - 1) as b:
                body(b, True, False)
            body(B - 1, True, True)

        block = ctx.enter_context(nc.Block())

        @block.sync
        def _(sp):
            sp.dma_start(cond_sb[:, :], cond).then_inc(cond_loaded, 16)
            sp.dma_start(wmod_raw, W_mod.rearrange("(c p) n -> p c n", p=P)).then_inc(wmod_loaded, 16)
            for b in range(B):
                sp.dma_start(x_all[:, b, :, :], x_tiles[:, b, :, :]).then_inc(x_loaded[b], 16)
            with nc.allow_non_contiguous_dma(reason="bias vectors to columns"):
                sp.dma_start(bmod_col[:, :], b_mod.rearrange("(k p) -> p k", p=P)).then_inc(small_loaded, 16)
                sp.dma_start(b1_col[:, :], b1.rearrange("(k p) -> p k", p=P)).then_inc(small_loaded, 16)
            for g, k in ((0, 2), (1, 5)):
                row = b_mod[k * D:(k + 1) * D].rearrange("(a n) -> a n", a=1)
                sp.dma_start(bmod_rep[:, g, :], row.to_broadcast([P, D])).then_inc(small_loaded, 16)
            for g, b_row in ((0, b_out), (1, b2)):
                for part in (0, 32):
                    sp.dma_start(bias_raw[part:part + 1, g, :], b_row.rearrange("(a n) -> a n", a=1)).then_inc(small_loaded, 16)
            sp.dma_start(wqkv_raw.rearrange("p (c n) -> p c n", c=DC),
                         W_qkv.rearrange("(c p) n -> p c n", p=P)).then_inc(wqkv_loaded, 16)
            sp.dma_start(wout_raw.rearrange("p (c n) -> p c n", c=PAIRS),
                         W_out.rearrange("(c p) n -> p c n", p=P)).then_inc(wrest_loaded, 16)
            sp.dma_start(w1_raw.rearrange("p (c n) -> p c n", c=DC),
                         W1.rearrange("(c p) n -> p c n", p=P)).then_inc(wrest_loaded, 16)
            sp.dma_start(w2_raw.rearrange("p (c n) -> p c n", c=FC),
                         W2.rearrange("(c p) n -> p c n", p=P)).then_inc(wrest_loaded, 16)

            def spread_k(ready, u):
                sp.wait_ge(k_hi_ready, ready)
                sp.wait_ge(k_lo_ready, ready)
                for h in range(2):
                    for half in range(2):
                        for src, dst in ((k_hi, k2_hi), (k_lo, k2_lo)):
                            sp.dma_start(dst[DH * half:DH * (half + 1), u, h, :],
                                         src[DH * h:DH * (h + 1), :]).then_inc(k_spread, 16)

            def spread_q(ready, u):
                sp.wait_ge(q_hi_ready, ready)
                sp.wait_ge(q_lo_ready, ready)
                for h in range(2):
                    for half, src in ((0, q_hi), (1, q_lo)):
                        sp.dma_start(q2[DH * half:DH * (half + 1), u, h, :],
                                     src[DH * h:DH * (h + 1), :]).then_inc(q_spread, 16)

            spread_k(1, 0)
            spread_q(1, 0)

            def pair(j, u):
                if exists(j, ahead=1):
                    spread_k(j + 2, 1 - u)
                    spread_q(j + 2, 1 - u)

            over_pairs(sp, pair)

            sp.wait_ge(vals_made, KC * NP)
            sp.dma_start(x_all, x_tiles).then_inc(xr_loaded, 16)

            def store(b, before, last):
                for half in range(2):
                    sp.wait_ge(y_ready, 2 * b + half + 1)
                    sp.dma_start(out_tiles[:, b, 2 * half:2 * half + 2, :],
                                 x_all[:, b, 2 * half:2 * half + 2, :]).then_inc(stored, 16)

            over_batches(sp, store)
            sp.wait_ge(stored, 16 * 2 * B)

        @block.gpsimd
        def _(pool):
            nc.gpsimd.memset(ident[:, :], 0.0).then_inc(wrest_step, 1)
            nc.gpsimd.memset(ones[:, :], 1.0)
            nc.gpsimd.memset(one[:, :], 1.0)
            nc.gpsimd.memset(bias_rows[:, :, :], 0.0)
            pool.wait_ge(wrest_step, 1)
            nc.gpsimd.affine_select(out=ident[:, :], in_=ident[:, :], compare_op=ALU.not_equal, fill=1.0, base=0,
                                    pattern=[[-1, P]], channel_multiplier=1).then_inc(consts_ready, 1)
            pool.wait_ge(wrest_loaded, 48)
            n = 1
            for raw, hi, lo in ((wout_raw, wout_hi, wout_lo), (w1_raw, w1_hi, w1_lo), (w2_raw, w2_hi, w2_lo)):
                flat_hi = hi[:, :, :].rearrange("p c n -> p (c n)")
                flat_lo = lo[:, :, :].rearrange("p c n -> p (c n)")
                nc.gpsimd.tensor_scalar(raw, raw, WS, None, ALU.mult).then_inc(wrest_step, 1)
                pool.wait_ge(wrest_step, n + 1)
                nc.gpsimd.tensor_copy(flat_hi, raw).then_inc(wrest_step, 1)
                pool.wait_ge(wrest_step, n + 2)
                nc.gpsimd.tensor_tensor(flat_lo, raw, flat_hi, ALU.subtract).then_inc(wrest_ready, 1)
                n += 2

            def pair(j, u):
                if exists(j, back=1):
                    pool.wait_ge(recip_ready, j)
                    if exists(j, back=2):
                        pool.wait_ge(recip_turned, j - 1)
                    nc.gpsimd.tensor_tensor(recip_rep[:, :, :, :].rearrange("p t h d -> p (t h) d"),
                                            recip[:, :, :].rearrange("p t h -> p (t h)").unsqueeze(2).to_broadcast([P, 2 * QT, DH]),
                                            one[:, :].unsqueeze(2).to_broadcast([P, 2 * QT, DH]),
                                            ALU.mult).then_inc(recip_rep_ready, 1)
                if exists(j, back=2):
                    n = j - 2
                    b, h = (n // PAIRS, n % PAIRS)
                    pool.wait_ge(o_norm_ready, j - 1)
                    nc.gpsimd.tensor_copy(o_hi[:, b, h, :], o_norm[:, u, :]).then_inc(o_hi_ready, 1)
                    pool.wait_ge(o_hi_ready, j - 1)
                    nc.gpsimd.tensor_tensor(o_lo[:, b, h, :], o_norm[:, u, :], o_hi[:, b, h, :], ALU.subtract).then_inc(o_lo_ready, 1)

            over_pairs(pool, pair)

        @block.scalar
        def _(act):
            act.wait_ge(cond_turned, 1)
            nc.scalar.activation(exp_c[:, :, :], ps_vals[:, 0:CC * B].rearrange("p (c b) -> p c b", c=CC), ACT.Exp,
                                 scale=-1.0).then_inc(exp_c_ready, 1)
            act.wait_ge(wqkv_loaded, 16)
            flat = wqkv_hi[:, :, :, :, :].rearrange("p c w h m -> p (c w h m)")
            part = DC * 3 * INNER // 4
            for i in range(4):
                nc.scalar.activation(flat[:, i * part:(i + 1) * part], wqkv_raw[:, i * part:(i + 1) * part], ACT.Copy,
                                     scale=WS).then_inc(wqkv_hi_ready, 1)
            act.wait_ge(small_loaded, 16 * 8)
            act.wait_ge(consts_ready, 1)
            nc.scalar.activation(bias_rows[0:1, :, :], bias_raw[0:1, :, :], ACT.Copy, scale=WS)
            nc.scalar.activation(bias_hi[32:33, :, :], bias_raw[32:33, :, :], ACT.Copy, scale=WS).then_inc(bias_hi_ready, 1)
            act.wait_ge(modT_ready, 1)
            for b in range(B):
                for c in range(DC):
                    n = b * DC + c
                    act.wait_ge(xn_turned, n + 1)
                    if n >= 2:
                        act.wait_ge(xnT_lo_ready, n - 1)
                    nc.scalar.activation(mod1[:, c, :], ps_turn[:, c, :], ACT.Identity, bias=modT[:, c, b:b + 1],
                                         scale=modT[:, DC + c, b:b + 1]).then_inc(mod1_ready, 1)
                    act.wait_ge(mod1_ready, n + 1)
                    nc.scalar.activation(xnT_hi[:, c, b, :], mod1[:, c, :], ACT.Copy).then_inc(xnT_hi_ready, 1)

            def k_part(n):
                act.wait_ge(k_made, n + 1)
                if exists(n, back=1):
                    act.wait_ge(k_spread, 128 * n)
                nc.scalar.activation(k_hi, ps_proj[:, :], ACT.Copy, scale=DH ** -0.5 / WS).then_inc(k_hi_ready, 1)

            def q_part(n):
                act.wait_ge(q_made, n + 1)
                if exists(n, back=1):
                    act.wait_ge(q_spread, 64 * n)
                nc.scalar.activation(q_hi, ps_proj[:, :], ACT.Copy, scale=1 / WS).then_inc(q_hi_ready, 1)

            def turn_part(s, u, qt, first_of_buffer):
                for h in range(2):
                    act.wait_ge(turned, 2 * s + h + 1)
                    nc.scalar.activation(probsT_hi[:, u, h, :, qt * P:(qt + 1) * P],
                                         ps_turn[:, h, :].rearrange("p (k q) -> p k q", k=KC),
                                         ACT.Copy).then_inc(turn_hi_ready, 1)

            k_part(0)
            q_part(0)

            def pair(j, u):
                for qt in range(QT):
                    s = QT * j + qt
                    back = 1 if qt < 2 else 0
                    if exists(j, back=back):
                        if qt == 2 and exists(j, back=2):
                            act.wait_ge(vals_made, KC * (j - 1))
                        turn_part(s - 2, u if qt >= 2 else 1 - u, (qt + 2) % QT, qt == 2)
                    if exists(j):
                        act.wait_ge(max_ready, s + 1)
                        for h in range(2):
                            e = nc.scalar.activation(probs[:, qt % 2, h, :], ps_scores[qt % 2][:, h, :], ACT.Exp,
                                                     bias=neg_max[:, qt % 2, h:h + 1],
                                                     accum_out=sums[:, u, qt, h:h + 1])
                        e.then_inc(probs_ready, 1)
                    if qt == 0 and exists(j, ahead=1):
                        k_part(j + 1)
                    if qt == 1 and exists(j, ahead=1):
                        q_part(j + 1)
                    if qt == 2 and exists(j, back=1):
                        act.wait_ge(recip_turned, j)
                        nc.scalar.activation(o_norm[:, 1 - u, :], ps_proj[:, :], ACT.Copy).then_inc(recip_T_ready, 1)
                    if qt == 3 and exists(j):
                        act.wait_ge(v_made, j + 1)
                        if exists(j, back=2):
                            act.wait_ge(vals_made, KC * (j - 1))
                        nc.scalar.activation(v_hi[:, u, :, :], ps_proj[:, :].rearrange("p (k m) -> p k m", k=KC), ACT.Copy,
                                             scale=1 / WS).then_inc(v_hi_ready, 1)

            over_pairs(act, pair)

            def batch(b, before, last):
                for c in range(DC):
                    act.wait_ge(xn2_turned, DC * b + c + 1)
                    if before:
                        act.wait_ge(xn2T_lo_ready, DC * b)
                    nc.scalar.activation(mod2[:, c, :], ps_turn[:, c, :], ACT.Identity, bias=modT[:, 4 + c, bass.ds(b, 1)],
                                         scale=modT[:, 4 + DC + c, bass.ds(b, 1)]).then_inc(mod2_ready, 1)
                    act.wait_ge(mod2_ready, DC * b + c + 1)
                    if before:
                        act.wait_ge(hid_made, FC * b)
                    nc.scalar.activation(xn2T_hi[:, c, :], mod2[:, c, :], ACT.Copy).then_inc(xn2T_hi_ready, 1)
                for f in range(FC):
                    act.wait_ge(hid_made, FC * b + f + 1)
                    if f >= 2:
                        act.wait_ge(h_lo_ready, FC * b + f - 1)
                    elif before:
                        act.wait_ge(h_lo_ready, FC * b)
                    nc.scalar.activation(gelu_out[:, f % 2, :], ps_hid[f % 2][:, :], ACT.Gelu, bias=b1_col[:, f:f + 1],
                                         scale=1 / WS).then_inc(gelu_ready, 1)
                    act.wait_ge(gelu_ready, FC * b + f + 1)
                    if f == 0:
                        if before:
                            act.wait_ge(mlp_made, 2 * b)
                    nc.scalar.activation(h_hi[:, f, :], gelu_out[:, f % 2, :], ACT.Copy).then_inc(h_hi_ready, 1)

            over_batches(act, batch)

        @block.vector
        def _(dve):
            count = [0]

            def link(ins, base=0):
                count[0] += 1
                ins.then_inc(dve_chain, 1)
                dve.wait_ge(dve_chain, base + count[0])

            def rsqrt(v, y, t, base=0):
                link(nc.vector.tensor_scalar(y.bitcast(I32), v.bitcast(I32), -0.5, RSQRT_MAGIC, ALU.mult, ALU.add), base)
                for _ in range(3):
                    link(nc.vector.tensor_tensor(t, y, y, ALU.mult), base)
                    link(nc.vector.scalar_tensor_tensor(out=t, in0=t, scalar=-0.5, in1=v, op0=ALU.mult, op1=ALU.mult), base)
                    link(nc.vector.scalar_tensor_tensor(out=y, in0=t, scalar=1.5, in1=y, op0=ALU.add, op1=ALU.mult), base)

            dve.wait_ge(exp_c_ready, 1)
            link(nc.vector.tensor_scalar(exp_c[:, :, :], exp_c[:, :, :], 1.0, None, ALU.add))
            link(nc.vector.reciprocal(exp_c[:, :, :], exp_c[:, :, :]))
            link(nc.vector.tensor_tensor(silu_c[:, :, :], exp_c[:, :, :],
                                         ps_vals[:, 0:CC * B].rearrange("p (c b) -> p c b", c=CC), ALU.mult))
            nc.vector.tensor_copy(silu_rep, silu_c[:, :, :].unsqueeze(3).to_broadcast([P, CC, B, P])).then_inc(silu_ready, 1)

            for b in range(B):
                dve.wait_ge(x_loaded[b], 16)
                for t in range(QT):
                    ins = nc.vector.bn_stats(stats[:, b * QT + t, :], x_all[:, b, t, :])
            link(ins)
            for t in range(NT):
                ins = nc.vector.bn_aggr(mv[:, t, :], stats[:, t, :])
            link(ins)
            link(nc.vector.tensor_scalar(var[:, :], mv[:, :, 1], EPS, None, ALU.add))
            rsqrt(var[:, :], rstd[:, :], newton[:, :])
            for b in range(B):
                for t in range(QT):
                    n = b * QT + t
                    ins = nc.vector.tensor_scalar(x_all[:, b, t, :], x_all[:, b, t, :], mv[:, n, 0:1], rstd[:, n:n + 1],
                                                  ALU.subtract, ALU.mult)
                ins.then_inc(xn_ready, 1)

            dve.wait_ge(small_loaded, 16 * 8)
            dve.wait_ge(mod_made, 1)
            made = ps_proj[:, 0:8 * B].rearrange("p (k b) -> p k b", b=B)
            for g in range(2):
                ins = nc.vector.tensor_tensor(modT[:, 4 * g:4 * g + 4, :], made[:, 4 * g:4 * g + 4, :],
                                              bmod_col[:, 6 * g:6 * g + 4].unsqueeze(2).to_broadcast([P, 4, B]), ALU.add)
            link(ins)
            for g in range(2):
                ins = nc.vector.tensor_scalar(modT[:, 4 * g + 2:4 * g + 4, :], modT[:, 4 * g + 2:4 * g + 4, :], 1.0, None, ALU.add)
            ins.then_inc(modT_ready, 1)
            dve.wait_ge(gates_made, 1)
            for b in range(B):
                ins = nc.vector.tensor_tensor(gates[:, b, :, :], ps_scores[b // 2][:, b % 2, :].rearrange("p (g d) -> p g d", g=2),
                                              bmod_rep, ALU.add)
            ins.then_inc(gates_read, 1)
            dve.wait_ge(gates_read, 1)
            nc.vector.tensor_scalar(gates[:, :, :, :], gates[:, :, :, :], 1 / WS, None, ALU.mult)

            flat_hi = wqkv_hi[:, :, :, :, :].rearrange("p c w h m -> p (c w h m)")
            flat_lo = wqkv_lo[:, :, :, :, :].rearrange("p c w h m -> p (c w h m)")
            part = DC * 3 * INNER // 4
            for i in range(4):
                dve.wait_ge(wqkv_hi_ready, i + 1)
                sl = slice(i * part, (i + 1) * part)
                nc.vector.scalar_tensor_tensor(out=flat_lo[:, sl], in0=wqkv_raw[:, sl], scalar=WS, in1=flat_hi[:, sl],
                                               op0=ALU.mult, op1=ALU.subtract).then_inc(wqkv_lo_ready, 1)
            dve.wait_ge(bias_hi_ready, 1)
            nc.vector.scalar_tensor_tensor(out=bias_rows[32:33, :, :], in0=bias_raw[32:33, :, :], scalar=WS,
                                           in1=bias_hi[32:33, :, :], op0=ALU.mult, op1=ALU.subtract).then_inc(bias_ready, 1)
            for b in range(B):
                for c in range(DC):
                    dve.wait_ge(xnT_hi_ready, b * DC + c + 1)
                    nc.vector.tensor_tensor(xnT_lo[:, c, b, :], mod1[:, c, :], xnT_hi[:, c, b, :],
                                            ALU.subtract).then_inc(xnT_lo_ready, 1)

            def lo_of(out, ps, scale, hi, done):
                nc.vector.scalar_tensor_tensor(out=out, in0=ps, scalar=scale, in1=hi, op0=ALU.mult,
                                               op1=ALU.subtract).then_inc(done, 1)

            def k_part(n):
                dve.wait_ge(k_hi_ready, n + 1)
                lo_of(k_lo, ps_proj[:, :], DH ** -0.5 / WS, k_hi, k_lo_ready)

            def q_part(n):
                dve.wait_ge(q_hi_ready, n + 1)
                lo_of(q_lo, ps_proj[:, :], 1 / WS, q_hi, q_lo_ready)

            k_part(0)
            q_part(0)

            def pair(j, u):
                for qt in range(QT):
                    s = QT * j + qt
                    if qt == 2 and exists(j, back=2):
                        dve.wait_ge(vals_made, KC * (j - 1))
                        dve.wait_ge(recip_T_ready, j - 1)
                        nc.vector.tensor_tensor(o_norm[:, u, :], ps_vals[:, :], o_norm[:, u, :], ALU.mult).then_inc(o_norm_ready, 1)
                    if exists(j):
                        dve.wait_ge(scores_made, s + 1)
                        nc.vector.tensor_reduce(neg_max[:, qt % 2, :], ps_scores[qt % 2][:, :, :], AX.X, ALU.max,
                                                negate=True).then_inc(max_ready, 1)
                    if exists(j, back=1 if qt < 2 else 0):
                        tu, tq = (u if qt >= 2 else 1 - u), (qt + 2) % QT
                        for h in range(2):
                            dve.wait_ge(turn_hi_ready, 2 * (s - 2) + h + 1)
                            nc.vector.tensor_tensor(probsT_lo[:, tu, h, :, tq * P:(tq + 1) * P],
                                                    ps_turn[:, h, :].rearrange("p (k q) -> p k q", k=KC),
                                                    probsT_hi[:, tu, h, :, tq * P:(tq + 1) * P],
                                                    ALU.subtract).then_inc(turn_lo_ready, 1)
                    if qt == 0 and exists(j, ahead=1):
                        k_part(j + 1)
                    if qt == 1 and exists(j, ahead=1):
                        q_part(j + 1)
                    if qt == 1 and exists(j, back=1):
                        dve.wait_ge(probs_ready, QT * j)
                        if exists(j, back=2):
                            dve.wait_ge(recip_rep_ready, j - 1)
                        nc.vector.reciprocal(recip[:, :, :], sums[:, 1 - u, :, :]).then_inc(recip_ready, 1)
                    if qt == 3 and exists(j):
                        dve.wait_ge(v_hi_ready, j + 1)
                        lo_of(v_lo[:, u, :, :], ps_proj[:, :].rearrange("p (k m) -> p k m", k=KC), 1 / WS, v_hi[:, u, :, :],
                              v_lo_ready)

            over_pairs(dve, pair)

            dve.wait_ge(xr_loaded, 16)
            LINKS = 2 + 1 + 1 + 1 + 10
            start = count[0]

            def batch(b, before, last):
                count[0] = start
                base = LINKS * b
                g_rows = [gates[:, b, g, :].unsqueeze(1).to_broadcast([P, 2, D]) for g in range(2)]
                if before:
                    dve.wait_ge(y_ready, 2 * b)
                for half in range(2):
                    dve.wait_ge(attn_made, 2 * b + half + 1)
                    ins = nc.vector.tensor_tensor(scaled[:, half, :, :], ps_attn[:, half, :, :], g_rows[0], ALU.mult)
                    ins.then_inc(attn_read, 1)
                dve.wait_ge(attn_read, 2 * b + 2)
                for half in range(2):
                    rows = x_all[:, b, 2 * half:2 * half + 2, :]
                    link(nc.vector.tensor_tensor(rows, rows, scaled[:, half, :, :], ALU.add), base)
                nc.vector.memset(wait_bearer[:, :], 0.0)
                for t in range(QT):
                    ins = nc.vector.bn_stats(stats[:, t, :], x_all[:, b, t, :])
                link(ins, base)
                nc.vector.memset(wait_bearer[:, :], 0.0)
                for t in range(QT):
                    ins = nc.vector.bn_aggr(mv[:, t, :], stats[:, t, :])
                link(ins, base)
                link(nc.vector.tensor_scalar(var[:, 0:QT], mv[:, 0:QT, 1], EPS, None, ALU.add), base)
                rsqrt(var[:, 0:QT], rstd[:, 0:QT], newton[:, 0:QT], base)
                if before:
                    dve.wait_ge(xn2_turned, DC * b)
                for t in range(QT):
                    ins = nc.vector.tensor_scalar(xn2[:, t, :], x_all[:, b, t, :], mv[:, t, 0:1], rstd[:, t:t + 1],
                                                  ALU.subtract, ALU.mult)
                ins.then_inc(xn2_ready, 1)
                for c in range(DC):
                    dve.wait_ge(xn2T_hi_ready, DC * b + c + 1)
                    nc.vector.tensor_tensor(xn2T_lo[:, c, :], mod2[:, c, :], xn2T_hi[:, c, :],
                                            ALU.subtract).then_inc(xn2T_lo_ready, 1)
                for f in range(FC):
                    dve.wait_ge(h_hi_ready, FC * b + f + 1)
                    nc.vector.tensor_tensor(h_lo[:, f, :], gelu_out[:, f % 2, :], h_hi[:, f, :],
                                            ALU.subtract).then_inc(h_lo_ready, 1)
                for half in range(2):
                    rows = x_all[:, b, 2 * half:2 * half + 2, :]
                    dve.wait_ge(mlp_made, 2 * b + half + 1)
                    nc.vector.tensor_tensor(scaled[:, half, :, :], ps_mlp[:, half, :, :], g_rows[1],
                                            ALU.mult).then_inc(mlp_read, 1)
                    dve.wait_ge(mlp_read, 2 * b + half + 1)
                    ins = nc.vector.tensor_tensor(rows, rows, scaled[:, half, :, :], ALU.add)
                    ins.then_inc(y_ready, 1)
                assert count[0] - start == LINKS

            over_batches(dve, batch)

        @block.tensor
        def _(pe):
            def split_product(out, w_hi, w_lo, m_hi, m_lo, first, last):
                nc.tensor.matmul(out, w_hi, m_hi, start=first, stop=False)
                nc.tensor.matmul(out, w_hi, m_lo, start=False, stop=False)
                return nc.tensor.matmul(out, w_lo, m_hi, start=False, stop=last)

            pe.wait_ge(cond_loaded, 16)
            pe.wait_ge(consts_ready, 1)
            for c in range(CC):
                ins = nc.tensor.transpose(ps_vals[:, c * B:(c + 1) * B], cond_sb[:, c * P:(c + 1) * P], ident[0:B, 0:B])
            ins.then_inc(cond_turned, 1)
            pe.wait_ge(silu_ready, 1)
            pe.wait_ge(wmod_loaded, 16)
            for g in range(2):
                for k in range(4):
                    col = (6 * g + k) * P
                    for c in range(CC):
                        ins = nc.tensor.matmul(ps_proj[:, (4 * g + k) * B:(4 * g + k + 1) * B],
                                               wmod_raw[:, c, col:col + P], silu_c[:, c, :],
                                               start=(c == 0), stop=(c == CC - 1))
            ins.then_inc(mod_made, 1)
            for b in range(B):
                for g, k in ((0, 2), (1, 5)):
                    for c in range(CC):
                        ins = nc.tensor.matmul(ps_scores[b // 2][:, b % 2, g * D:(g + 1) * D], silu_rep[:, c, b, :],
                                               wmod_raw[:, c, k * D:(k + 1) * D], start=(c == 0), stop=(c == CC - 1))
            ins.then_inc(gates_made, 1)
            for b in range(B):
                pe.wait_ge(xn_ready, b + 1)
                for c in range(DC):
                    n = b * DC + c
                    if n >= 2:
                        pe.wait_ge(mod1_ready, n - 1)
                    for t in range(QT):
                        ins = nc.tensor.transpose(ps_turn[:, c, t * P:(t + 1) * P], x_all[:, b, t, c * P:(c + 1) * P], ident[:, :])
                    ins.then_inc(xn_turned, 1)

            def head_slices(n):
                return n // PAIRS, n % PAIRS

            def project(which, n, done):
                b, h = head_slices(n)
                for c in range(DC):
                    ins = split_product(ps_proj[:, :], wqkv_hi[:, c, which, h, :], wqkv_lo[:, c, which, h, :],
                                        xnT_hi[:, c, b, :], xnT_lo[:, c, b, :], c == 0, c == DC - 1)
                ins.then_inc(done, 1)

            def project_v(n, done):
                b, h = head_slices(n)
                for k in range(KC):
                    sl = slice(k * P, (k + 1) * P)
                    for c in range(DC):
                        ins = split_product(ps_proj[:, sl], xnT_hi[:, c, b, sl], xnT_lo[:, c, b, sl],
                                            wqkv_hi[:, c, 2, h, :], wqkv_lo[:, c, 2, h, :], c == 0, c == DC - 1)
                ins.then_inc(done, 1)

            def values(k, u):
                for i, (v, p) in enumerate(((v_hi, probsT_hi), (v_hi, probsT_lo), (v_lo, probsT_hi))):
                    for h in range(2):
                        ins = nc.tensor.matmul(ps_vals[DH * h:DH * (h + 1), :], v[:, u, k, DH * h:DH * (h + 1)],
                                               p[:, u, h, k, :], start=(k == 0 and i == 0), stop=(k == KC - 1 and i == 2))
                ins.then_inc(vals_made, 1)

            pe.wait_ge(xnT_lo_ready, B * DC)
            pe.wait_ge(wqkv_lo_ready, 4)
            pe.wait_ge(gates_read, 1)
            project(1, 0, k_made)
            pe.wait_ge(k_lo_ready, 1)
            project(0, 0, q_made)

            def pair(j, u):
                for qt in range(QT):
                    s = QT * j + qt
                    if exists(j):
                        if qt == 0:
                            pe.wait_ge(k_spread, 128 * (j + 1))
                            pe.wait_ge(q_spread, 64 * (j + 1))
                        if qt >= 2 or exists(j, back=1):
                            pe.wait_ge(probs_ready, s - 1)
                        for h in range(2):
                            for k2 in (k2_hi, k2_lo):
                                ins = nc.tensor.matmul(ps_scores[qt % 2][:, h, :], q2[:, u, h, qt * P:(qt + 1) * P],
                                                       k2[:, u, h, :], start=(k2 is k2_hi), stop=(k2 is k2_lo))
                        ins.then_inc(scores_made, 1)
                    if exists(j, back=1 if qt < 2 else 0):
                        pe.wait_ge(probs_ready, s - 1)
                        for h in range(2):
                            if qt != 2 or exists(j, back=1):
                                pe.wait_ge(turn_lo_ready, 2 * (s - 3) + h + 1)
                            for k in range(KC):
                                ins = nc.tensor.transpose(ps_turn[:, h, k * P:(k + 1) * P],
                                                          probs[:, qt % 2, h, k * P:(k + 1) * P], ident[:, :])
                            ins.then_inc(turned, 1)
                    if qt == 0:
                        if exists(j, ahead=1):
                            if exists(j, back=1):
                                pe.wait_ge(v_lo_ready, j)
                            else:
                                pe.wait_ge(q_lo_ready, 1)
                            project(1, j + 1, k_made)
                        if exists(j, back=2):
                            values(2, u)
                    if qt == 1:
                        if exists(j, ahead=1):
                            pe.wait_ge(k_lo_ready, j + 2)
                            project(0, j + 1, q_made)
                        if exists(j, back=2):
                            values(3, u)
                    if qt == 2 and exists(j, back=1):
                        pe.wait_ge(turn_lo_ready, 2 * QT * j)
                        pe.wait_ge(v_lo_ready, j)
                        if exists(j, back=2):
                            pe.wait_ge(o_norm_ready, j - 1)
                        values(0, 1 - u)
                        pe.wait_ge(recip_rep_ready, j)
                        pe.wait_ge(q_lo_ready, (j if isinstance(j, int) and j >= NP - 1 else j + 1) + 1 if exists(j, ahead=1) else NP)
                        if not exists(j):
                            pe.wait_ge(v_lo_ready, NP)
                        for t in range(QT):
                            ins = nc.tensor.transpose(ps_proj[:, t * P:(t + 1) * P],
                                                      recip_rep[:, t, :, :].rearrange("p h d -> p (h d)"), ident[:, :])
                        ins.then_inc(recip_turned, 1)
                    if qt == 3:
                        if exists(j):
                            if exists(j, back=1):
                                pe.wait_ge(recip_T_ready, j)
                            elif exists(j, ahead=1):
                                pe.wait_ge(q_lo_ready, j + 2)
                            project_v(j, v_made)
                        if exists(j, back=1):
                            values(1, 1 - u)

            over_pairs(pe, pair)

            def attn_out(b):
                pe.wait_ge(o_lo_ready, PAIRS * (b + 1))
                for half in range(2):
                    if not isinstance(b, int) or b > 0:
                        pe.wait_ge(attn_read, 2 * b)
                    for t in range(2):
                        tok = slice((2 * half + t) * P, (2 * half + t + 1) * P)
                        o = ps_attn[:, half, t, :]
                        nc.tensor.matmul(o, ones[:, :], bias_rows[:, 0, :], start=True, stop=False)
                        for h in range(PAIRS):
                            ins = split_product(o, o_hi[:, b, h, tok], o_lo[:, b, h, tok], wout_hi[:, h, :], wout_lo[:, h, :],
                                                False, h == PAIRS - 1)
                    ins.then_inc(attn_made, 1)

            pe.wait_ge(recip_T_ready, NP)
            pe.wait_ge(o_norm_ready, NP)
            pe.wait_ge(wrest_ready, 3)
            pe.wait_ge(bias_ready, 1)
            attn_out(0)

            def batch(b, before, last):
                pe.wait_ge(xn2_ready, b + 1)
                for c in range(DC):
                    if before:
                        pe.wait_ge(mod2_ready, DC * b)
                    for t in range(QT):
                        ins = nc.tensor.transpose(ps_turn[:, c, t * P:(t + 1) * P], xn2[:, t, c * P:(c + 1) * P], ident[:, :])
                    ins.then_inc(xn2_turned, 1)
                pe.wait_ge(xn2T_lo_ready, DC * (b + 1))
                for f in range(FC):
                    if f >= 2:
                        pe.wait_ge(gelu_ready, FC * b + f - 1)
                    elif before:
                        pe.wait_ge(gelu_ready, FC * b)
                    for c in range(DC):
                        sl = slice(f * P, (f + 1) * P)
                        ins = split_product(ps_hid[f % 2][:, :], w1_hi[:, c, sl], w1_lo[:, c, sl], xn2T_hi[:, c, :],
                                            xn2T_lo[:, c, :], c == 0, c == DC - 1)
                    ins.then_inc(hid_made, 1)
                if not last:
                    attn_out(b + 1)
                pe.wait_ge(h_lo_ready, FC * (b + 1))
                if before:
                    pe.wait_ge(mlp_read, 2 * b)
                for half in range(2):
                    for t in range(2):
                        tok = slice((2 * half + t) * P, (2 * half + t + 1) * P)
                        o = ps_mlp[:, half, t, :]
                        nc.tensor.matmul(o, ones[:, :], bias_rows[:, 1, :], start=True, stop=False)
                        for f in range(FC):
                            ins = split_product(o, h_hi[:, f, tok], h_lo[:, f, tok], w2_hi[:, f, :], w2_lo[:, f, :],
                                                False, f == FC - 1)
                    ins.then_inc(mlp_made, 1)

            over_batches(pe, batch)


_INS = ['x', 'cond_1024', 'L0_cond_W_mod', 'L0_cond_b_mod', 'L0_cond_W_qkv', 'L0_cond_W_out', 'L0_cond_b_out',
        'L0_cond_W1', 'L0_cond_b1', 'L0_cond_W2', 'L0_cond_b2']
_OUTS = [((4, 512, 256), 'float32')]


def kernel(**inputs):
    import numpy as _np
    import concourse.bacc as _bacc
    from concourse import mybir as _mybir
    from concourse.bass_utils import run_bass_kernel_spmd as _run

    nc = _bacc.Bacc("TRN2", target_bir_lowering=False, num_devices=1)
    arrays, args = {}, []
    for name in _INS:
        a = _np.ascontiguousarray(inputs[name])
        arrays[f"in_{name}_dram"] = a
        args.append(nc.dram_tensor(f"in_{name}_dram", a.shape, _mybir.dt.from_np(a.dtype), kind="ExternalInput").ap())
    for i, (shape, dtype) in enumerate(_OUTS):
        dt = _mybir.dt.from_np(_np.dtype(dtype))
        args.append(nc.dram_tensor(f"out_{i}_dram", shape, dt, kind="ExternalOutput").ap())
    dit_block_kernel(nc, *args)
    r = _run(nc, [arrays], core_ids=[0])
    got = tuple(r.results[0][f"out_{i}_dram"] for i in range(len(_OUTS)))
    return got[0]
```

```python
from contextlib import ExitStack

import concourse.bass as bass
from concourse import mybir

F32 = mybir.dt.float32
F16 = mybir.dt.float16
I32 = mybir.dt.int32
ACT = mybir.ActivationFunctionType
ALU = mybir.AluOpType
AX = mybir.AxisListType

P = 128
EPS = 1e-5
WS = 64.0
RSQRT_MAGIC = 1597463007.0


def dit_block_kernel(nc, x, cond, W_mod, b_mod, W_qkv, W_out, b_out, W1, b1, W2, b2, out):
    B, T, D = x.shape
    COND = cond.shape[1]
    INNER = W_out.shape[0]
    MLP = W1.shape[1]
    DH = 64
    PAIRS = INNER // (2 * DH)
    NP = B * PAIRS
    QT = T // P
    KC = T // P
    DC = D // P
    CC = COND // P
    FC = MLP // P
    NT = B * QT
    assert T == 512 and D == 256 and COND == 256 and 2 * DH == P and QT == 4

    x_tiles = x.rearrange("b (t p) d -> p b t d", p=P)
    out_tiles = out.rearrange("b (t p) d -> p b t d", p=P)

    with ExitStack() as ctx:
        def sb(name, shape, dt):
            return ctx.enter_context(nc.sbuf_tensor(name, shape, dt))

        def sem(name):
            return ctx.enter_context(nc.semaphore(name))

        wqkv = sb("wqkv", [P, 2, DC * 3, PAIRS, P], F16)
        wqkv_hi = wqkv[:, 0, :, :, :].rearrange("p (c w) h m -> p c w h m", c=DC)
        wqkv_lo = wqkv[:, 1, :, :, :].rearrange("p (c w) h m -> p c w h m", c=DC)
        x_res = wqkv[:, :, :, :, :].rearrange("p a c h m -> p (a c h m)").bitcast(F32)[:, 0:NT * D].rearrange(
            "p (b t d) -> p b t d", b=B, t=QT)
        wout_hi = sb("wout_hi", [P, PAIRS, D], F16)
        wout_lo = sb("wout_lo", [P, PAIRS, D], F16)
        w1_hi = sb("w1_hi", [P, DC, MLP], F16)
        w1_lo = sb("w1_lo", [P, DC, MLP], F16)
        w2_hi = sb("w2_hi", [P, FC, D], F16)
        w2_lo = sb("w2_lo", [P, FC, D], F16)
        bias_rows = sb("bias_rows", [P, 2, D], F16)
        ones = sb("ones", [P, P], F16)
        ident = sb("ident", [P, P], F32)
        gates = sb("gates", [P, B, 2, D], F32)
        modT = sb("modT", [P, 8, B], F32)
        b1_col = sb("b1_col", [P, FC], F32)
        bmod_col = sb("bmod_col", [P, 6 * DC], F32)
        xnT_hi = sb("xnT_hi", [P, DC, B, T], F16)
        xnT_lo = sb("xnT_lo", [P, DC, B, T], F16)
        stats = sb("stats", [P, NT, 6], F32)
        mv = sb("mv", [P, NT, 2], F32)
        var = sb("var", [P, NT], F32)
        rstd = sb("rstd", [P, NT], F32)
        newton = sb("newton", [P, NT], F32)
        cond_sb = sb("cond_sb", [B, COND], F32)
        exp_c = sb("exp_c", [P, CC, B], F32)
        silu_c = sb("silu_c", [P, CC, B], F32)
        wait_bearer = sb("wait_bearer", [P, 1], F32)
        recip = sb("recip", [P, QT, 2], F32)
        one = sb("one", [P, 1], F32)
        w_scale = sb("w_scale", [P, 1], F32)
        neg_max = sb("neg_max", [P, 2, 2], F32)
        sums = sb("sums", [P, 2, QT, 2], F32)

        r1 = sb("r1", [P, 2 * NP * T], F16)
        o_hi = r1[:, 0:NP * T].rearrange("p (b h t) -> p b h t", b=B, h=PAIRS)
        o_lo = r1[:, NP * T:2 * NP * T].rearrange("p (b h t) -> p b h t", b=B, h=PAIRS)
        r1f = r1[:, :].bitcast(F32)
        at = [0]

        def stage(n):
            at[0] += n
            return r1f[:, at[0] - n:at[0]]

        wqkv_raw = stage(DC * 3 * INNER).rearrange("p (c h m) -> p c h m", c=DC * 3, h=PAIRS)
        wmod_raw = stage(CC * 6 * D).rearrange("p (c n) -> p c n", c=CC)
        wout_raw = stage(PAIRS * D)
        w1_raw = stage(DC * MLP)
        w2_raw = stage(FC * D)
        mod1 = stage(2 * T).rearrange("p (u t) -> p u t", u=2)

        r2 = sb("r2", [P, 2, 2, 2 * KC * T], F16)
        probsT_hi = r2[:, :, 0, :].rearrange("p u (h k q) -> p u h k q", h=2, k=KC)
        probsT_lo = r2[:, :, 1, :].rearrange("p u (h k q) -> p u h k q", h=2, k=KC)
        r2_temp = r2[:, 0, :, :].rearrange("p a n -> p (a n)").bitcast(F32)
        x_all = r2[:, 1, :, :].rearrange("p a n -> p (a n)").bitcast(F32).rearrange("p (b t d) -> p b t d", b=B, t=QT)
        silu_rep = r2_temp[:, 0:CC * B * P].rearrange("p (c b m) -> p c b m", c=CC, b=B)
        bmod_rep = r2_temp[:, 2 * T:3 * T].rearrange("p (g d) -> p g d", g=2)
        bias_raw = r2_temp[:, 3 * T:4 * T].rearrange("p (g d) -> p g d", g=2)
        bias_hi = r2_temp[:, 4 * T:5 * T].bitcast(F16)[:, 0:2 * D].rearrange("p (g d) -> p g d", g=2)
        h_hi = r2[:, 0, 0, :].rearrange("p (f t) -> p f t", f=FC)
        h_lo = r2[:, 0, 1, :].rearrange("p (f t) -> p f t", f=FC)

        r3 = sb("r3", [P, 2, 2, T], F32)
        probs = r3
        mod2 = r3[:, 0, :, :]
        gelu_out = r3[:, 1, :, :]

        r4 = sb("r4", [P, 16 * T], F16)
        q2 = r4[:, 0:4 * T].rearrange("p (u h t) -> p u h t", u=2, h=2)
        k2 = r4[:, 4 * T:12 * T].rearrange("p (u a h t) -> p u a h t", u=2, a=2, h=2)
        k_parts = r4[:, 12 * T:14 * T].rearrange("p (a t) -> p a t", a=2)
        k_hi, k_lo = k_parts[:, 0, :], k_parts[:, 1, :]
        q_hi, q_lo = r4[:, 14 * T:15 * T], r4[:, 15 * T:16 * T]
        r4f = r4[:, :].bitcast(F32)
        xn2 = r4f[:, 0:2 * T].rearrange("p (t d) -> p t d", t=QT)
        scaled = r4f[:, 2 * T:4 * T].rearrange("p (h t d) -> p h t d", h=2, t=2)
        xn2T_hi = r4[:, 8 * T:10 * T].rearrange("p (c t) -> p c t", c=DC)
        xn2T_lo = r4[:, 10 * T:12 * T].rearrange("p (c t) -> p c t", c=DC)

        v_hi = sb("v_hi", [P, KC, 2, P], F16)
        v_lo = sb("v_lo", [P, KC, 2, P], F16)
        recip_rep = sb("recip_rep", [P, QT, 2, DH], F32)
        o_norm = sb("o_norm", [P, 2, T], F32)

        ps_scores = [ctx.enter_context(nc.psum_tensor(f"ps_scores{i}", [P, 2, T], F32)) for i in range(2)]
        ps_turn = ctx.enter_context(nc.psum_tensor("ps_turn", [P, 2, T], F32))
        ps_proj = ctx.enter_context(nc.psum_tensor("ps_proj", [P, T], F32))
        ps_vals = ctx.enter_context(nc.psum_tensor("ps_vals", [P, T], F32))
        ps_attn = ps_scores[0][:, :, :].rearrange("p k (t d) -> p k t d", t=2)
        ps_mlp = ps_scores[1][:, :, :].rearrange("p k (t d) -> p k t d", t=2)
        ps_hid = [ps_proj, ps_vals]

        cond_loaded = sem("cond_loaded")
        wmod_loaded = [sem("wmod_first_loaded"), sem("wmod_loaded")]
        x_loaded = [sem(f"x_loaded{b}") for b in range(B)]
        wqkv_loaded = [sem("wqkv_first_loaded"), sem("wqkv_loaded")]
        wrest_loaded = [sem(f"wrest{i}_loaded") for i in range(3)]
        wrest_hi_ready = sem("wrest_hi_ready")
        bmod_loaded = sem("bmod_loaded")
        b1_loaded = sem("b1_loaded")
        small_loaded = sem("small_loaded")
        consts_ready = sem("consts_ready")
        cond_turned = sem("cond_turned")
        exp_c_ready = sem("exp_c_ready")
        silu_ready = sem("silu_ready")
        mod_made = sem("mod_made")
        modT_ready = sem("modT_ready")
        gates_made = sem("gates_made")
        gates_read = sem("gates_read")
        xn_ready = sem("xn_ready")
        xn_turned = sem("xn_turned")
        mod1_ready = sem("mod1_ready")
        xnT_hi_ready = sem("xnT_hi_ready")
        xnT_lo_ready = sem("xnT_lo_ready")
        wqkv_hi_ready = sem("wqkv_hi_ready")
        wqkv_lo_ready = sem("wqkv_lo_ready")
        wrest_step = sem("wrest_step")
        wrest_ready = sem("wrest_ready")
        bias_hi_ready = sem("bias_hi_ready")
        bias_ready = sem("bias_ready")
        dve_chain = sem("dve_chain")
        k_made, k_hi_ready, k_lo_ready, k_spread = (sem(n) for n in ("k_made", "k_hi_ready", "k_lo_ready", "k_spread"))
        q_made, q_hi_ready, q_lo_ready, q_spread = (sem(n) for n in ("q_made", "q_hi_ready", "q_lo_ready", "q_spread"))
        v_made, v_hi_ready, v_lo_ready = (sem(n) for n in ("v_made", "v_hi_ready", "v_lo_ready"))
        scores_made = sem("scores_made")
        max_ready = sem("max_ready")
        probs_ready = sem("probs_ready")
        turned = sem("turned")
        turn_hi_ready = sem("turn_hi_ready")
        turn_lo_ready = sem("turn_lo_ready")
        vals_made = sem("vals_made")
        recip_ready = sem("recip_ready")
        recip_rep_ready = sem("recip_rep_ready")
        recip_turned = sem("recip_turned")
        recip_T_ready = sem("recip_T_ready")
        o_norm_ready = sem("o_norm_ready")
        o_hi_ready = sem("o_hi_ready")
        o_lo_ready = sem("o_lo_ready")
        xr_loaded = sem("xr_loaded")
        attn_made = sem("attn_made")
        attn_read = sem("attn_read")
        xn2_ready = sem("xn2_ready")
        xn2_turned = sem("xn2_turned")
        mod2_ready = sem("mod2_ready")
        xn2T_hi_ready = sem("xn2T_hi_ready")
        xn2T_lo_ready = sem("xn2T_lo_ready")
        hid_made = sem("hid_made")
        gelu_ready = sem("gelu_ready")
        h_hi_ready = sem("h_hi_ready")
        h_lo_ready = sem("h_lo_ready")
        mlp_made = sem("mlp_made")
        mlp_read = sem("mlp_read")
        y_ready = sem("y_ready")
        stored = sem("stored")

        FIRST = 4
        WQKV_HI_SLOTS = (1, 4, 7, 9, 11, 13)
        WQKV_LO_SLOTS = (2, 6, 8, 10, 12, 14)
        WREST_SLOTS = (6, 9, 12)

        def over_pairs(eng, pair):
            for j in range(FIRST):
                pair(j, j % 2)
            with eng.Fori(FIRST // 2, NP // 2 - 1) as i:
                pair(2 * i, 0)
                pair(2 * i + 1, 1)
            for j in (NP - 2, NP - 1, NP, NP + 1):
                pair(j, j % 2)

        def exists(j, back=0, ahead=0):
            return not isinstance(j, int) or 0 <= j - back + ahead < NP

        def over_batches(eng, body):
            body(0, False, False)
            with eng.Fori(1, B - 1) as b:
                body(b, True, False)
            body(B - 1, True, True)

        block = ctx.enter_context(nc.Block())

        @block.sync
        def _(sp):
            wmod_dram = W_mod.rearrange("(c p) n -> p c n", p=P)
            wqkv_dram = W_qkv.rearrange("(c p) (w h m) -> p c w (h m)", p=P, w=3, h=PAIRS)
            wqkv_dst = wqkv_raw.rearrange("p (c w) h m -> p c w (h m)", c=DC)
            sp.dma_start(cond_sb[:, :], cond).then_inc(cond_loaded, 16)
            sp.dma_start(x_all[:, 0, :, :], x_tiles[:, 0, :, :]).then_inc(x_loaded[0], 16)
            sp.dma_start(wmod_raw[:, :, 0:2 * D], wmod_dram[:, :, 0:2 * D]).then_inc(wmod_loaded[0], 16)
            with nc.allow_non_contiguous_dma(reason="bias vector to columns"):
                sp.dma_start(bmod_col[:, :], b_mod.rearrange("(k p) -> p k", p=P)).then_inc(bmod_loaded, 16)
            for c in range(DC):
                sp.dma_start(wqkv_dst[:, c, :, 0:2 * P], wqkv_dram[:, c, :, 0:2 * P]).then_inc(wqkv_loaded[0], 16)
            sp.dma_start(wmod_raw[:, :, 2 * D:6 * D], wmod_dram[:, :, 2 * D:6 * D]).then_inc(wmod_loaded[1], 16)
            for g, k in ((0, 2), (1, 5)):
                row = b_mod[k * D:(k + 1) * D].rearrange("(a n) -> a n", a=1)
                sp.dma_start(bmod_rep[:, g, :], row.to_broadcast([P, D])).then_inc(small_loaded, 16)
            for g, b_row in ((0, b_out), (1, b2)):
                for part in (0, 32):
                    sp.dma_start(bias_raw[part:part + 1, g, :], b_row.rearrange("(a n) -> a n", a=1)).then_inc(small_loaded, 16)
            for b in range(1, B):
                sp.dma_start(x_all[:, b, :, :], x_tiles[:, b, :, :]).then_inc(x_loaded[b], 16)

            def spread_k(ready, u):
                sp.wait_ge(k_hi_ready, ready)
                sp.wait_ge(k_lo_ready, ready)
                for h in range(2):
                    for half in range(2):
                        sp.dma_start(k2[DH * half:DH * (half + 1), u, :, h, :],
                                     k_parts[DH * h:DH * (h + 1), :, :]).then_inc(k_spread, 16)

            def spread_q(ready, u):
                sp.wait_ge(q_hi_ready, ready)
                sp.wait_ge(q_lo_ready, ready)
                for h in range(2):
                    for half, src in ((0, q_hi), (1, q_lo)):
                        sp.dma_start(q2[DH * half:DH * (half + 1), u, h, :],
                                     src[DH * h:DH * (h + 1), :]).then_inc(q_spread, 16)

            spread_k(1, 0)
            spread_q(1, 0)
            for c in range(DC):
                sp.dma_start(wqkv_dst[:, c, :, 2 * P:], wqkv_dram[:, c, :, 2 * P:]).then_inc(wqkv_loaded[1], 16)
            for i, (raw, w, n) in enumerate(((wout_raw, W_out, PAIRS), (w1_raw, W1, DC), (w2_raw, W2, FC))):
                sp.dma_start(raw.rearrange("p (c n) -> p c n", c=n),
                             w.rearrange("(c p) n -> p c n", p=P)).then_inc(wrest_loaded[i], 16)
            with nc.allow_non_contiguous_dma(reason="bias vector to columns"):
                sp.dma_start(b1_col[:, :], b1.rearrange("(k p) -> p k", p=P)).then_inc(b1_loaded, 16)

            def pair(j, u):
                if exists(j, ahead=1):
                    spread_k(j + 2, 1 - u)
                    spread_q(j + 2, 1 - u)

            over_pairs(sp, pair)

            sp.wait_ge(v_made, NP)
            sp.dma_start(x_res, x_tiles).then_inc(xr_loaded, 16)

            def store(b, before, last):
                for half in range(2):
                    sp.wait_ge(y_ready, 2 * b + half + 1)
                    sp.dma_start(out_tiles[:, b, 2 * half:2 * half + 2, :],
                                 x_res[:, b, 2 * half:2 * half + 2, :]).then_inc(stored, 16)

            over_batches(sp, store)
            sp.wait_ge(stored, 16 * 2 * B)

        @block.gpsimd
        def _(pool):
            nc.gpsimd.memset(ident[:, :], 0.0).then_inc(wrest_step, 1)
            nc.gpsimd.memset(ones[:, :], 1.0)
            nc.gpsimd.memset(one[:, :], 1.0)
            nc.gpsimd.memset(w_scale[:, :], WS)
            nc.gpsimd.memset(bias_rows[:, :, :], 0.0)
            pool.wait_ge(wrest_step, 1)
            nc.gpsimd.affine_select(out=ident[:, :], in_=ident[:, :], compare_op=ALU.not_equal, fill=1.0, base=0,
                                    pattern=[[-1, P]], channel_multiplier=1).then_inc(consts_ready, 1)
            def wrest_part(i):
                raw, hi, lo = ((wout_raw, wout_hi, wout_lo), (w1_raw, w1_hi, w1_lo), (w2_raw, w2_hi, w2_lo))[i]
                pool.wait_ge(wrest_hi_ready, i + 1)
                nc.gpsimd.tensor_tensor(raw, raw, w_scale[:, :].to_broadcast([P, PAIRS * D]), ALU.mult).then_inc(wrest_step, 1)
                pool.wait_ge(wrest_step, i + 2)
                nc.gpsimd.tensor_tensor(lo[:, :, :].rearrange("p c n -> p (c n)"), raw, hi[:, :, :].rearrange("p c n -> p (c n)"),
                                        ALU.subtract).then_inc(wrest_ready, 1)

            def pair(j, u):
                if exists(j, back=1):
                    pool.wait_ge(recip_ready, j)
                    if exists(j, back=2):
                        pool.wait_ge(recip_turned, j - 1)
                    nc.gpsimd.tensor_tensor(recip_rep[:, :, :, :].rearrange("p t h d -> p (t h) d"),
                                            recip[:, :, :].rearrange("p t h -> p (t h)").unsqueeze(2).to_broadcast([P, 2 * QT, DH]),
                                            one[:, :].unsqueeze(2).to_broadcast([P, 2 * QT, DH]),
                                            ALU.mult).then_inc(recip_rep_ready, 1)
                if exists(j, back=2):
                    n = j - 2
                    b, h = (n // PAIRS, n % PAIRS)
                    pool.wait_ge(o_norm_ready, j - 1)
                    nc.gpsimd.tensor_copy(o_hi[:, b, h, :], o_norm[:, u, :]).then_inc(o_hi_ready, 1)
                    pool.wait_ge(o_hi_ready, j - 1)
                    nc.gpsimd.tensor_tensor(o_lo[:, b, h, :], o_norm[:, u, :], o_hi[:, b, h, :], ALU.subtract).then_inc(o_lo_ready, 1)
                if isinstance(j, int) and 1 <= j < FIRST:
                    wrest_part(j - 1)

            over_pairs(pool, pair)

        @block.scalar
        def _(act):
            act.wait_ge(cond_turned, 1)
            nc.scalar.activation(exp_c[:, :, :], ps_vals[:, 0:CC * B].rearrange("p (c b) -> p c b", c=CC), ACT.Exp,
                                 scale=-1.0).then_inc(exp_c_ready, 1)

            def wqkv_part(h0, h1):
                nc.scalar.activation(wqkv[:, 0, :, h0:h1, :], wqkv_raw[:, :, h0:h1, :], ACT.Copy,
                                     scale=WS).then_inc(wqkv_hi_ready, 1)

            def modulate(b, c, made):
                n = b * DC + c
                act.wait_ge(xn_turned, n + 1)
                if n >= 2:
                    act.wait_ge(xnT_lo_ready, n - 1)
                nc.scalar.activation(mod1[:, c, :], made, ACT.Identity, bias=modT[:, c, b:b + 1],
                                     scale=modT[:, DC + c, b:b + 1]).then_inc(mod1_ready, 1)
                act.wait_ge(mod1_ready, n + 1)
                nc.scalar.activation(xnT_hi[:, c, b, :], mod1[:, c, :], ACT.Copy).then_inc(xnT_hi_ready, 1)

            act.wait_ge(wqkv_loaded[0], 16 * DC)
            wqkv_part(0, 2)
            act.wait_ge(modT_ready, 1)
            for c in range(DC):
                modulate(0, c, ps_turn[:, c, :])

            def k_part(n):
                act.wait_ge(k_made, n + 1)
                if exists(n, back=1):
                    act.wait_ge(k_spread, 64 * n)
                nc.scalar.activation(k_hi, ps_proj[:, :], ACT.Copy, scale=DH ** -0.5 / WS).then_inc(k_hi_ready, 1)

            def q_part(n, made=ps_proj):
                act.wait_ge(q_made, n + 1)
                if exists(n, back=1):
                    act.wait_ge(q_spread, 64 * n)
                nc.scalar.activation(q_hi, made[:, :], ACT.Copy, scale=1 / WS).then_inc(q_hi_ready, 1)

            def turn_part(s, u, qt):
                for h in range(2):
                    act.wait_ge(turned, 2 * s + h + 1)
                    nc.scalar.activation(probsT_hi[:, u, h, :, qt * P:(qt + 1) * P],
                                         ps_turn[:, h, :].rearrange("p (k q) -> p k q", k=KC),
                                         ACT.Copy).then_inc(turn_hi_ready, 1)

            k_part(0)
            q_part(0, ps_vals)
            act.wait_ge(small_loaded, 16 * 6)
            act.wait_ge(consts_ready, 1)
            nc.scalar.activation(bias_rows[0:1, :, :], bias_raw[0:1, :, :], ACT.Copy, scale=WS)
            nc.scalar.activation(bias_hi[32:33, :, :], bias_raw[32:33, :, :], ACT.Copy, scale=WS).then_inc(bias_hi_ready, 1)

            def start_part(i):
                if i < DC * (B - 1):
                    modulate(1 + i // DC, i % DC, ps_vals[:, :])
                if i in WQKV_HI_SLOTS:
                    n = WQKV_HI_SLOTS.index(i)
                    if n == 0:
                        act.wait_ge(wqkv_loaded[1], 16 * DC)
                    wqkv_part(n + 2, n + 3)
                if i in WREST_SLOTS:
                    n = WREST_SLOTS.index(i)
                    raw, hi = ((wout_raw, wout_hi), (w1_raw, w1_hi), (w2_raw, w2_hi))[n]
                    act.wait_ge(wrest_loaded[n], 16)
                    nc.scalar.activation(hi[:, :, :].rearrange("p c n -> p (c n)"), raw, ACT.Copy,
                                         scale=WS).then_inc(wrest_hi_ready, 1)

            def pair(j, u):
                for qt in range(QT):
                    s = QT * j + qt
                    back = 1 if qt < 2 else 0
                    if exists(j, back=back):
                        if qt == 2 and exists(j, back=2):
                            act.wait_ge(vals_made, KC * (j - 1))
                        turn_part(s - 2, u if qt >= 2 else 1 - u, (qt + 2) % QT)
                    if qt == 0 and exists(j, ahead=1):
                        k_part(j + 1)
                    if qt == 1 and exists(j, ahead=1):
                        q_part(j + 1)
                    if qt == 3 and exists(j):
                        act.wait_ge(v_made, j + 1)
                        if exists(j, back=2):
                            act.wait_ge(vals_made, KC * (j - 1) + (2 if u == 0 else 0))
                        nc.scalar.activation(v_hi[:, 2 * u:2 * u + 2, :, :],
                                             ps_proj[:, :].rearrange("p (k w m) -> p k w m", k=2, w=2), ACT.Copy,
                                             scale=1 / WS).then_inc(v_hi_ready, 1)
                    if qt == 2 and exists(j, back=1):
                        act.wait_ge(recip_turned, j)
                        nc.scalar.activation(o_norm[:, 1 - u, :], ps_proj[:, :], ACT.Copy).then_inc(recip_T_ready, 1)
                    if exists(j):
                        act.wait_ge(max_ready, s + 1)
                        for h in range(2):
                            e = nc.scalar.activation(probs[:, qt % 2, h, :], ps_scores[qt % 2][:, h, :], ACT.Exp,
                                                     bias=neg_max[:, qt % 2, h:h + 1],
                                                     accum_out=sums[:, u, qt, h:h + 1])
                        e.then_inc(probs_ready, 1)
                    if isinstance(j, int) and j < FIRST:
                        start_part(s)

            over_pairs(act, pair)

            def modulate2(b, before):
                for c in range(DC):
                    act.wait_ge(xn2_turned, DC * b + c + 1)
                    if before:
                        act.wait_ge(xn2T_lo_ready, DC * b)
                        act.wait_ge(hid_made, FC * b)
                    nc.scalar.activation(mod2[:, c, :], ps_turn[:, c, :], ACT.Identity, bias=modT[:, 4 + c, bass.ds(b, 1)],
                                         scale=modT[:, 4 + DC + c, bass.ds(b, 1)]).then_inc(mod2_ready, 1)
                    act.wait_ge(mod2_ready, DC * b + c + 1)
                    nc.scalar.activation(xn2T_hi[:, c, :], mod2[:, c, :], ACT.Copy).then_inc(xn2T_hi_ready, 1)

            modulate2(0, False)
            act.wait_ge(b1_loaded, 16)

            def batch(b, before, last):
                for f in range(FC):
                    act.wait_ge(hid_made, FC * b + f + 1)
                    if f >= 2:
                        act.wait_ge(h_lo_ready, FC * b + f - 1)
                    elif before:
                        act.wait_ge(h_lo_ready, FC * b)
                    nc.scalar.activation(gelu_out[:, f % 2, :], ps_hid[f % 2][:, :], ACT.Gelu, bias=b1_col[:, f:f + 1],
                                         scale=1 / WS).then_inc(gelu_ready, 1)
                    act.wait_ge(gelu_ready, FC * b + f + 1)
                    if f == 0 and before:
                        act.wait_ge(mlp_made, 2 * b)
                    nc.scalar.activation(h_hi[:, f, :], gelu_out[:, f % 2, :], ACT.Copy).then_inc(h_hi_ready, 1)
                if not last:
                    modulate2(b + 1, True)

            over_batches(act, batch)

        @block.vector
        def _(dve):
            count = [0]

            def link(ins, base=0):
                count[0] += 1
                ins.then_inc(dve_chain, 1)
                dve.wait_ge(dve_chain, base + count[0])

            def rsqrt(v, y, t, base=0):
                link(nc.vector.tensor_scalar(y.bitcast(I32), v.bitcast(I32), -0.5, RSQRT_MAGIC, ALU.mult, ALU.add), base)
                for _ in range(3):
                    link(nc.vector.tensor_tensor(t, y, y, ALU.mult), base)
                    link(nc.vector.scalar_tensor_tensor(out=t, in0=t, scalar=-0.5, in1=v, op0=ALU.mult, op1=ALU.mult), base)
                    link(nc.vector.scalar_tensor_tensor(out=y, in0=t, scalar=1.5, in1=y, op0=ALU.add, op1=ALU.mult), base)

            dve.wait_ge(exp_c_ready, 1)
            link(nc.vector.tensor_scalar(exp_c[:, :, :], exp_c[:, :, :], 1.0, None, ALU.add))
            link(nc.vector.reciprocal(exp_c[:, :, :], exp_c[:, :, :]))
            link(nc.vector.tensor_tensor(silu_c[:, :, :], exp_c[:, :, :],
                                         ps_vals[:, 0:CC * B].rearrange("p (c b) -> p c b", c=CC), ALU.mult))
            nc.vector.tensor_copy(silu_rep, silu_c[:, :, :].unsqueeze(3).to_broadcast([P, CC, B, P])).then_inc(silu_ready, 1)

            def moments(b):
                dve.wait_ge(x_loaded[b], 16)
                for t in range(QT):
                    ins = nc.vector.bn_stats(stats[:, b * QT + t, :], x_all[:, b, t, :])
                return ins

            def statistics(first, end, made):
                t0, t1 = first * QT, end * QT
                link(made)
                for t in range(t0, t1):
                    ins = nc.vector.bn_aggr(mv[:, t, :], stats[:, t, :])
                link(ins)
                link(nc.vector.tensor_scalar(var[:, t0:t1], mv[:, t0:t1, 1], EPS, None, ALU.add))
                rsqrt(var[:, t0:t1], rstd[:, t0:t1], newton[:, t0:t1])

            def normalise(b):
                for t in range(QT):
                    n = b * QT + t
                    ins = nc.vector.tensor_scalar(x_all[:, b, t, :], x_all[:, b, t, :], mv[:, n, 0:1], rstd[:, n:n + 1],
                                                  ALU.subtract, ALU.mult)
                ins.then_inc(xn_ready, 1)

            def columns(g, made):
                dve.wait_ge(mod_made, g + 1)
                dve.wait_ge(bmod_loaded, 16)
                link(nc.vector.tensor_tensor(modT[:, 4 * g:4 * g + 4, :], made.rearrange("p (k b) -> p k b", b=B),
                                             bmod_col[:, 6 * g:6 * g + 4].unsqueeze(2).to_broadcast([P, 4, B]), ALU.add))
                nc.vector.tensor_scalar(modT[:, 4 * g + 2:4 * g + 4, :], modT[:, 4 * g + 2:4 * g + 4, :], 1.0, None,
                                        ALU.add).then_inc(modT_ready, 1)

            def gate_rows(b):
                dve.wait_ge(gates_made, b + 1)
                nc.vector.tensor_tensor(gates[:, b, :, :], ps_scores[b // 2][:, b % 2, :].rearrange("p (g d) -> p g d", g=2),
                                        bmod_rep, ALU.add).then_inc(gates_read, 1)

            def wqkv_part(h0, h1, n):
                dve.wait_ge(wqkv_hi_ready, n)
                for c in range(DC * 3):
                    ins = nc.vector.scalar_tensor_tensor(out=wqkv[:, 1, c, h0:h1, :], in0=wqkv_raw[:, c, h0:h1, :], scalar=WS,
                                                         in1=wqkv[:, 0, c, h0:h1, :], op0=ALU.mult, op1=ALU.subtract)
                ins.then_inc(wqkv_lo_ready, 1)

            def modulated_lo(b, c):
                dve.wait_ge(xnT_hi_ready, b * DC + c + 1)
                nc.vector.tensor_tensor(xnT_lo[:, c, b, :], mod1[:, c, :], xnT_hi[:, c, b, :],
                                        ALU.subtract).then_inc(xnT_lo_ready, 1)

            statistics(0, 1, moments(0))
            normalise(0)
            columns(0, ps_proj[:, 0:4 * B])
            wqkv_part(0, 2, 1)
            for c in range(DC):
                modulated_lo(0, c)

            def lo_of(out, ps, scale, hi, done):
                nc.vector.scalar_tensor_tensor(out=out, in0=ps, scalar=scale, in1=hi, op0=ALU.mult,
                                               op1=ALU.subtract).then_inc(done, 1)

            def k_part(n):
                dve.wait_ge(k_hi_ready, n + 1)
                lo_of(k_lo, ps_proj[:, :], DH ** -0.5 / WS, k_hi, k_lo_ready)

            def q_part(n, made=ps_proj):
                dve.wait_ge(q_hi_ready, n + 1)
                lo_of(q_lo, made[:, :], 1 / WS, q_hi, q_lo_ready)

            moments(1)
            moments(2)
            k_part(0)
            made = moments(3)
            q_part(0, ps_vals)
            dve.wait_ge(small_loaded, 16 * 6)
            gate_rows(0)
            gate_rows(1)
            dve.wait_ge(bias_hi_ready, 1)
            nc.vector.scalar_tensor_tensor(out=bias_rows[32:33, :, :], in0=bias_raw[32:33, :, :], scalar=WS,
                                           in1=bias_hi[32:33, :, :], op0=ALU.mult, op1=ALU.subtract).then_inc(bias_ready, 1)
            gate_rows(2)
            statistics(1, B, made)
            gate_rows(3)
            normalise(1)

            def start_part(i):
                if i < DC * (B - 1):
                    modulated_lo(1 + i // DC, i % DC)
                if i < 2:
                    normalise(2 + i)
                if i == 2:
                    columns(1, ps_proj[:, 0:4 * B])
                if i in WQKV_LO_SLOTS:
                    n = WQKV_LO_SLOTS.index(i)
                    wqkv_part(n + 2, n + 3, n + 2)

            def pair(j, u):
                for qt in range(QT):
                    s = QT * j + qt
                    if qt == 2 and exists(j, back=2):
                        dve.wait_ge(vals_made, KC * (j - 1))
                        dve.wait_ge(recip_T_ready, j - 1)
                        nc.vector.tensor_tensor(o_norm[:, u, :], ps_vals[:, :], o_norm[:, u, :], ALU.mult).then_inc(o_norm_ready, 1)
                    if exists(j):
                        dve.wait_ge(scores_made, s + 1)
                        nc.vector.tensor_reduce(neg_max[:, qt % 2, :], ps_scores[qt % 2][:, :, :], AX.X, ALU.max,
                                                negate=True).then_inc(max_ready, 1)
                    if isinstance(j, int) and 0 < s < QT * FIRST:
                        start_part(s - 1)
                    if exists(j, back=1 if qt < 2 else 0):
                        tu, tq = (u if qt >= 2 else 1 - u), (qt + 2) % QT
                        for h in range(2):
                            dve.wait_ge(turn_hi_ready, 2 * (s - 2) + h + 1)
                            nc.vector.tensor_tensor(probsT_lo[:, tu, h, :, tq * P:(tq + 1) * P],
                                                    ps_turn[:, h, :].rearrange("p (k q) -> p k q", k=KC),
                                                    probsT_hi[:, tu, h, :, tq * P:(tq + 1) * P],
                                                    ALU.subtract).then_inc(turn_lo_ready, 1)
                    if qt == 0 and exists(j, back=1):
                        dve.wait_ge(probs_ready, QT * j)
                        if exists(j, back=2):
                            dve.wait_ge(recip_rep_ready, j - 1)
                        nc.vector.reciprocal(recip[:, :, :], sums[:, 1 - u, :, :]).then_inc(recip_ready, 1)
                    if qt == 0 and exists(j, ahead=1):
                        k_part(j + 1)
                    if qt == 1 and exists(j, ahead=1):
                        q_part(j + 1)
                    if qt == 3 and exists(j):
                        dve.wait_ge(v_hi_ready, j + 1)
                        lo_of(v_lo[:, 2 * u:2 * u + 2, :, :], ps_proj[:, :].rearrange("p (k w m) -> p k w m", k=2, w=2), 1 / WS,
                              v_hi[:, 2 * u:2 * u + 2, :, :], v_lo_ready)
                    if isinstance(j, int) and j == NP and qt == QT - 1:
                        dve.wait_ge(xr_loaded, 16)
                        start[0] = count[0]
                        residual(0, 0, False)
                        layernorm(0, residual(0, 1, False), False)

            LINKS = 2 + 1 + 1 + 1 + 10
            start = [0]

            def gate_row(b, g):
                return gates[:, b, g, :].unsqueeze(1).to_broadcast([P, 2, D])

            def residual(b, half, before):
                base = LINKS * b
                if half == 0:
                    count[0] = start[0]
                dve.wait_ge(attn_made, 2 * b + half + 1)
                if before:
                    if not isinstance(b, int) or b > 1:
                        dve.wait_ge(y_ready, 2 * b + half - 3)
                    else:
                        dve.wait_ge(dve_chain, base + start[0])
                nc.vector.tensor_tensor(scaled[:, half, :, :], ps_attn[:, half, :, :], gate_row(b, 0), ALU.mult).then_inc(attn_read, 1)
                dve.wait_ge(attn_read, 2 * b + half + 1)
                rows = x_res[:, b, 2 * half:2 * half + 2, :]
                link(nc.vector.scalar_tensor_tensor(out=rows, in0=scaled[:, half, :, :], scalar=1 / WS, in1=rows,
                                                    op0=ALU.mult, op1=ALU.add), base)
                nc.vector.memset(wait_bearer[:, :], 0.0)
                for t in (2 * half, 2 * half + 1):
                    ins = nc.vector.bn_stats(stats[:, t, :], x_res[:, b, t, :])
                return ins

            def layernorm(b, stats_made, before):
                base = LINKS * b
                link(stats_made, base)
                nc.vector.memset(wait_bearer[:, :], 0.0)
                for t in range(QT):
                    ins = nc.vector.bn_aggr(mv[:, t, :], stats[:, t, :])
                link(ins, base)
                link(nc.vector.tensor_scalar(var[:, 0:QT], mv[:, 0:QT, 1], EPS, None, ALU.add), base)
                rsqrt(var[:, 0:QT], rstd[:, 0:QT], newton[:, 0:QT], base)
                if before:
                    dve.wait_ge(xn2_turned, DC * b)
                for t in range(QT):
                    ins = nc.vector.tensor_scalar(xn2[:, t, :], x_res[:, b, t, :], mv[:, t, 0:1], rstd[:, t:t + 1],
                                                  ALU.subtract, ALU.mult)
                ins.then_inc(xn2_ready, 1)
                assert count[0] - start[0] == LINKS

            def layernorm_lo(b):
                for c in range(DC):
                    dve.wait_ge(xn2T_hi_ready, DC * b + c + 1)
                    nc.vector.tensor_tensor(xn2T_lo[:, c, :], mod2[:, c, :], xn2T_hi[:, c, :],
                                            ALU.subtract).then_inc(xn2T_lo_ready, 1)

            def output(b, half, last):
                rows = x_res[:, b, 2 * half:2 * half + 2, :]
                dve.wait_ge(mlp_made, 2 * b + half + 1)
                if last:
                    dve.wait_ge(y_ready, 2 * b + half - 1)
                nc.vector.tensor_tensor(scaled[:, half, :, :], ps_mlp[:, half, :, :], gate_row(b, 1),
                                        ALU.mult).then_inc(mlp_read, 1)
                dve.wait_ge(mlp_read, 2 * b + half + 1)
                nc.vector.scalar_tensor_tensor(out=rows, in0=scaled[:, half, :, :], scalar=1 / WS, in1=rows,
                                               op0=ALU.mult, op1=ALU.add).then_inc(y_ready, 1)

            over_pairs(dve, pair)
            layernorm_lo(0)

            def batch(b, before, last):
                if not last:
                    residual(b + 1, 0, True)
                for f in range(FC):
                    dve.wait_ge(h_hi_ready, FC * b + f + 1)
                    nc.vector.tensor_tensor(h_lo[:, f, :], gelu_out[:, f % 2, :], h_hi[:, f, :],
                                            ALU.subtract).then_inc(h_lo_ready, 1)
                if not last:
                    layernorm(b + 1, residual(b + 1, 1, True), True)
                output(b, 0, last)
                if not last:
                    layernorm_lo(b + 1)
                output(b, 1, last)

            over_batches(dve, batch)

        @block.tensor
        def _(pe):
            def split_product(out, w_hi, w_lo, m_hi, m_lo, first, last):
                nc.tensor.matmul(out, w_hi, m_hi, start=first, stop=False)
                nc.tensor.matmul(out, w_hi, m_lo, start=False, stop=False)
                return nc.tensor.matmul(out, w_lo, m_hi, start=False, stop=last)

            pe.wait_ge(cond_loaded, 16)
            pe.wait_ge(consts_ready, 1)
            for c in range(CC):
                ins = nc.tensor.transpose(ps_vals[:, c * B:(c + 1) * B], cond_sb[:, c * P:(c + 1) * P], ident[0:B, 0:B])
            ins.then_inc(cond_turned, 1)
            def columns(g):
                for k in range(4):
                    col = (6 * g + k) * P
                    for c in range(CC):
                        ins = nc.tensor.matmul(ps_proj[:, k * B:(k + 1) * B], wmod_raw[:, c, col:col + P], silu_c[:, c, :],
                                               start=(c == 0), stop=(c == CC - 1))
                ins.then_inc(mod_made, 1)

            def gate_rows(b):
                for g, k in ((0, 2), (1, 5)):
                    for c in range(CC):
                        ins = nc.tensor.matmul(ps_scores[b // 2][:, b % 2, g * D:(g + 1) * D], silu_rep[:, c, b, :],
                                               wmod_raw[:, c, k * D:(k + 1) * D], start=(c == 0), stop=(c == CC - 1))
                ins.then_inc(gates_made, 1)

            def turn_layernorm(b, c, to):
                for t in range(QT):
                    ins = nc.tensor.transpose(to[:, t * P:(t + 1) * P], x_all[:, b, t, c * P:(c + 1) * P], ident[:, :])
                ins.then_inc(xn_turned, 1)

            pe.wait_ge(silu_ready, 1)
            pe.wait_ge(wmod_loaded[0], 16)
            columns(0)
            pe.wait_ge(xn_ready, 1)
            for c in range(DC):
                turn_layernorm(0, c, ps_turn[:, c, :])

            def head_slices(n):
                return n // PAIRS, n % PAIRS

            def project(which, n, done, to=ps_proj):
                b, h = head_slices(n)
                for c in range(DC):
                    ins = split_product(to[:, :], wqkv_hi[:, c, which, h, :], wqkv_lo[:, c, which, h, :],
                                        xnT_hi[:, c, b, :], xnT_lo[:, c, b, :], c == 0, c == DC - 1)
                ins.then_inc(done, 1)

            def project_v(j, u, done):
                b, h = head_slices(j - u)
                for i in range(2):
                    k = 2 * u + i
                    sl = slice(k * P, (k + 1) * P)
                    for c in range(DC):
                        w_hi, w_lo = (w[:, c, 2, bass.ds(h, 2), :] for w in (wqkv_hi, wqkv_lo))
                        ins = split_product(ps_proj[:, i * 2 * P:(i + 1) * 2 * P].rearrange("p (w m) -> p w m", w=2),
                                            xnT_hi[:, c, b, sl], xnT_lo[:, c, b, sl], w_hi, w_lo, c == 0, c == DC - 1)
                ins.then_inc(done, 1)

            def values(k, u):
                for i, (v, p) in enumerate(((v_hi, probsT_hi), (v_hi, probsT_lo), (v_lo, probsT_hi))):
                    for h in range(2):
                        ins = nc.tensor.matmul(ps_vals[DH * h:DH * (h + 1), :], v[:, k, u, DH * h:DH * (h + 1)],
                                               p[:, u, h, k, :], start=(k == 0 and i == 0), stop=(k == KC - 1 and i == 2))
                ins.then_inc(vals_made, 1)

            pe.wait_ge(wmod_loaded[1], 16)
            gate_rows(0)
            pe.wait_ge(modT_ready, 1)
            pe.wait_ge(wqkv_lo_ready, 1)
            pe.wait_ge(xnT_lo_ready, DC)
            project(1, 0, k_made)
            project(0, 0, q_made, ps_vals)
            for b in range(1, B):
                gate_rows(b)

            def start_part(i):
                if i < DC * (B - 1):
                    b = 1 + i // DC
                    pe.wait_ge(xn_ready, b + 1)
                    if i > 0:
                        pe.wait_ge(mod1_ready, DC + i)
                    turn_layernorm(b, i % DC, ps_vals[:, :])
                if i == 2:
                    pe.wait_ge(q_lo_ready, 2)
                    columns(1)

            def pair(j, u):
                for qt in range(QT):
                    s = QT * j + qt
                    if exists(j):
                        if qt == 0:
                            pe.wait_ge(k_spread, 64 * (j + 1))
                            pe.wait_ge(q_spread, 64 * (j + 1))
                        if qt >= 2 or exists(j, back=1):
                            pe.wait_ge(probs_ready, s - 1)
                        else:
                            pe.wait_ge(gates_read, 2 * (s + 1))
                        for h in range(2):
                            for a in range(2):
                                ins = nc.tensor.matmul(ps_scores[qt % 2][:, h, :], q2[:, u, h, qt * P:(qt + 1) * P],
                                                       k2[:, u, a, h, :], start=(a == 0), stop=(a == 1))
                        ins.then_inc(scores_made, 1)
                    if exists(j, back=1 if qt < 2 else 0):
                        pe.wait_ge(probs_ready, s - 1)
                        for h in range(2):
                            if qt != 2 or exists(j, back=1):
                                pe.wait_ge(turn_lo_ready, 2 * (s - 3) + h + 1)
                            for k in range(KC):
                                ins = nc.tensor.transpose(ps_turn[:, h, k * P:(k + 1) * P],
                                                          probs[:, qt % 2, h, k * P:(k + 1) * P], ident[:, :])
                            ins.then_inc(turned, 1)
                    if qt == 0:
                        if exists(j, ahead=1):
                            if exists(j, back=1):
                                pe.wait_ge(v_lo_ready, j)
                            else:
                                pe.wait_ge(k_lo_ready, 1)
                            if isinstance(j, int) and 1 <= j < FIRST:
                                pe.wait_ge(wqkv_lo_ready, j + 1)
                            project(1, j + 1, k_made)
                        if exists(j, back=2):
                            if not exists(j):
                                pe.wait_ge(v_lo_ready, NP)
                            values(2, u)
                    if qt == 1:
                        if exists(j, ahead=1):
                            pe.wait_ge(k_lo_ready, j + 2)
                            project(0, j + 1, q_made)
                        if exists(j, back=2):
                            values(3, u)
                    if qt == 2 and exists(j, back=1):
                        pe.wait_ge(recip_rep_ready, j)
                        pe.wait_ge(q_lo_ready, j + 2 if exists(j, ahead=1) else NP)
                        if not exists(j):
                            pe.wait_ge(v_lo_ready, NP)
                        for t in range(QT):
                            ins = nc.tensor.transpose(ps_proj[:, t * P:(t + 1) * P],
                                                      recip_rep[:, t, :, :].rearrange("p h d -> p (h d)"), ident[:, :])
                        ins.then_inc(recip_turned, 1)
                        pe.wait_ge(turn_lo_ready, 2 * QT * j)
                        pe.wait_ge(v_lo_ready, j)
                        if isinstance(j, int) and j == 1:
                            pe.wait_ge(xnT_lo_ready, DC * B)
                        if exists(j, back=2):
                            pe.wait_ge(o_norm_ready, j - 1)
                        values(0, 1 - u)
                    if qt == 3:
                        if exists(j, back=1):
                            values(1, 1 - u)
                        if exists(j):
                            if exists(j, back=1):
                                pe.wait_ge(recip_T_ready, j)
                            else:
                                pe.wait_ge(modT_ready, 2)
                            project_v(j, u, v_made)
                    if isinstance(j, int) and j < FIRST:
                        start_part(s)
                    if isinstance(j, int) and j == FIRST - 1 and qt == 3:
                        pe.wait_ge(wqkv_lo_ready, PAIRS - 1)
                    if isinstance(j, int) and j == NP and qt < 2:
                        attn_out(0, 2 * qt)
                        attn_out(0, 2 * qt + 1)

            def attn_out(b, tile):
                half, t = tile // 2, tile % 2
                if tile == 0:
                    pe.wait_ge(o_lo_ready, PAIRS * (b + 1))
                    if isinstance(b, int) and b == 0:
                        pe.wait_ge(wrest_ready, 3)
                        pe.wait_ge(bias_ready, 1)
                if t == 0 and not (isinstance(b, int) and b == 0):
                    pe.wait_ge(attn_read, 2 * b + half - 1)
                tok = slice(tile * P, (tile + 1) * P)
                o = ps_attn[:, half, t, :]
                nc.tensor.matmul(o, ones[:, :], bias_rows[:, 0, :], start=True, stop=False)
                for h in range(PAIRS):
                    ins = split_product(o, o_hi[:, b, h, tok], o_lo[:, b, h, tok], wout_hi[:, h, :], wout_lo[:, h, :],
                                        False, h == PAIRS - 1)
                if t == 1:
                    ins.then_inc(attn_made, 1)

            over_pairs(pe, pair)

            def turn_layernorm2(b, before):
                pe.wait_ge(xn2_ready, b + 1)
                if before:
                    pe.wait_ge(mod2_ready, DC * b)
                for c in range(DC):
                    for t in range(QT):
                        ins = nc.tensor.transpose(ps_turn[:, c, t * P:(t + 1) * P], xn2[:, t, c * P:(c + 1) * P], ident[:, :])
                    ins.then_inc(xn2_turned, 1)

            attn_out(1, 0)
            attn_out(1, 1)
            turn_layernorm2(0, False)
            attn_out(1, 2)
            pe.wait_ge(recip_T_ready, NP)
            pe.wait_ge(o_norm_ready, NP)

            def mlp_out(b, tile, before):
                half, t = tile // 2, tile % 2
                if t == 0 and before:
                    pe.wait_ge(mlp_read, 2 * b + half - 1)
                tok = slice(tile * P, (tile + 1) * P)
                o = ps_mlp[:, half, t, :]
                nc.tensor.matmul(o, ones[:, :], bias_rows[:, 1, :], start=True, stop=False)
                for f in range(FC):
                    ins = split_product(o, h_hi[:, f, tok], h_lo[:, f, tok], w2_hi[:, f, :], w2_lo[:, f, :],
                                        False, f == FC - 1)
                if t == 1:
                    ins.then_inc(mlp_made, 1)

            def batch(b, before, last):
                if before and not last:
                    attn_out(b + 1, 0)
                    attn_out(b + 1, 1)
                pe.wait_ge(xn2T_lo_ready, DC * (b + 1))
                for f in range(FC):
                    if f >= 2:
                        pe.wait_ge(gelu_ready, FC * b + f - 1)
                    elif before:
                        pe.wait_ge(gelu_ready, FC * b)
                    for c in range(DC):
                        sl = slice(f * P, (f + 1) * P)
                        ins = split_product(ps_hid[f % 2][:, :], w1_hi[:, c, sl], w1_lo[:, c, sl], xn2T_hi[:, c, :],
                                            xn2T_lo[:, c, :], c == 0, c == DC - 1)
                    ins.then_inc(hid_made, 1)
                if not last:
                    if before:
                        attn_out(b + 1, 2)
                    attn_out(b + 1, 3)
                pe.wait_ge(h_lo_ready, FC * (b + 1))
                for tile in range(QT):
                    if tile == QT - 1 and not last:
                        turn_layernorm2(b + 1, True)
                    mlp_out(b, tile, before)

            over_batches(pe, batch)


_INS = ['x', 'cond_1024', 'L0_cond_W_mod', 'L0_cond_b_mod', 'L0_cond_W_qkv', 'L0_cond_W_out', 'L0_cond_b_out',
        'L0_cond_W1', 'L0_cond_b1', 'L0_cond_W2', 'L0_cond_b2']
_OUTS = [((4, 512, 256), 'float32')]


def kernel(**inputs):
    import numpy as _np
    import concourse.bacc as _bacc
    from concourse import mybir as _mybir
    from concourse.bass_utils import run_bass_kernel_spmd as _run

    nc = _bacc.Bacc("TRN2", target_bir_lowering=False, num_devices=1)
    arrays, args = {}, []
    for name in _INS:
        a = _np.ascontiguousarray(inputs[name])
        arrays[f"in_{name}_dram"] = a
        args.append(nc.dram_tensor(f"in_{name}_dram", a.shape, _mybir.dt.from_np(a.dtype), kind="ExternalInput").ap())
    for i, (shape, dtype) in enumerate(_OUTS):
        dt = _mybir.dt.from_np(_np.dtype(dtype))
        args.append(nc.dram_tensor(f"out_{i}_dram", shape, dt, kind="ExternalOutput").ap())
    dit_block_kernel(nc, *args)
    r = _run(nc, [arrays], core_ids=[0])
    got = tuple(r.results[0][f"out_{i}_dram"] for i in range(len(_OUTS)))
    return got[0]
```
